# Optimizing a Trainium2 kernel written in Bass

```python
import numpy as np
import jax
import jax.numpy as jnp

def _softmax(x, axis=-1):
    return jax.nn.softmax(x, axis=axis)

def _gelu(x):
    return jax.nn.gelu(x, approximate=True)

def _silu(x):
    return jax.nn.silu(x)

def _sigmoid(x):
    return jax.nn.sigmoid(x)

def _layernorm(x, axis=-1, eps=1e-05):
    m = jnp.mean(x, axis=axis, keepdims=True)
    v = jnp.var(x, axis=axis, keepdims=True)
    return (x - m) / jnp.sqrt(v + eps)

def _scatter_add(tgt, idx, src, axis=0):
    return tgt.at[idx].add(src)

def _segment_sum(src, seg, n):
    return jax.ops.segment_sum(src, seg, n)
kernel_name = 'mk_gnn_resnorm_d2_gnn_r8_9bbbae'

def setup_inputs(seed: int=0):
    np.random.seed(seed)
    _w = jnp.asarray

    def _rec_inputs():
        import jax
        import jax.numpy as jnp
        _gk = jax.random.key(seed)
        x = -0.0003713 + 1 * jax.random.normal(jax.random.fold_in(_gk, 1), (12500, 128), jnp.float32)
        _s = jax.random.randint(jax.random.fold_in(_gk, 2), (100000,), 0, 12500, jnp.int32)
        _d = jax.random.randint(jax.random.fold_in(_gk, 3), (100000,), 0, 12500, jnp.int32)
        _loop = jnp.arange(12500, dtype=jnp.int32)
        src = jnp.concatenate([_s, _d, _loop])
        dst = jnp.concatenate([_d, _s, _loop])
        _o = jnp.argsort(dst, stable=True)
        src = src[_o]
        dst = dst[_o]
        edge_type_8 = jax.random.randint(jax.random.fold_in(_gk, 13), (212500,), 0, 8, jnp.int32)
        return (x, src, dst, edge_type_8)
    x, src, dst, edge_type_8 = _rec_inputs()

    def _L0_gnn_setup():
        import jax, jax.numpy as jnp
        import numpy as np
        N_ENT = 12500

        def _rgcn_layer(x, W, SW, b, src, dst, rel):
            xt = jnp.einsum('nd,rde->rne', x, W)
            msg = xt[rel, src]
            agg = jax.ops.segment_sum(msg, dst, num_segments=x.shape[0])
            return jax.nn.relu(agg + x @ SW + b)
        key = jax.random.key(seed)
        ks = jax.random.split(key, 8)
        d, R, E = (128, 8, 75000)
        scale = 1.0 / np.sqrt(d)
        return {'entity_emb': jax.random.normal(ks[0], (N_ENT, d), dtype=jnp.float32), 'w1': jax.random.normal(ks[1], (R, d, d), dtype=jnp.float32) * scale, 'sl1': jax.random.normal(ks[2], (d, d), dtype=jnp.float32) * scale, 'b1': jnp.zeros((d,), dtype=jnp.float32), 'w2': jax.random.normal(ks[3], (R, d, d), dtype=jnp.float32) * scale, 'sl2': jax.random.normal(ks[4], (d, d), dtype=jnp.float32) * scale, 'b2': jnp.zeros((d,), dtype=jnp.float32), 'edge_index': jax.random.randint(ks[5], (2, E), 0, N_ENT, dtype=jnp.int64), 'edge_type': jax.random.randint(ks[6], (E,), 0, R, dtype=jnp.int64)}
    _L0_gnn_all = _L0_gnn_setup()
    _L0_gnn_in = {k: v for k, v in _L0_gnn_all.items() if k in ('w1', 'sl1', 'b1', 'w2', 'sl2', 'b2')}
    del _L0_gnn_all

    def _L1_gnn_setup():
        import jax, jax.numpy as jnp
        import numpy as np
        N_NODES = 12500
        N_EDGES = 400000
        D_IN = 128
        D_HID = 128
        D_OUT = 128
        key = jax.random.key(seed)
        ks = jax.random.split(key, 7)
        x = jax.random.normal(ks[0], (N_NODES, D_IN), dtype=jnp.float32)
        src = jax.random.randint(ks[1], (N_EDGES,), 0, N_NODES, dtype=jnp.int32)
        dst = jax.random.randint(ks[2], (N_EDGES,), 0, N_NODES, dtype=jnp.int32)
        W1 = jax.random.normal(ks[3], (D_IN, D_HID), dtype=jnp.float32) * D_IN ** (-0.5)
        b1 = jax.random.normal(ks[4], (D_HID,), dtype=jnp.float32) * 0.01
        W2 = jax.random.normal(ks[5], (D_HID, D_OUT), dtype=jnp.float32) * D_HID ** (-0.5)
        b2 = jax.random.normal(ks[6], (D_OUT,), dtype=jnp.float32) * 0.01
        return {'x': x, 'src': src, 'dst': dst, 'W1': W1, 'b1': b1, 'W2': W2, 'b2': b2}
    _L1_gnn_all = _L1_gnn_setup()
    _L1_gnn_in = {k: v for k, v in _L1_gnn_all.items() if k in ('W1', 'b1', 'W2', 'b2')}
    del _L1_gnn_all
    return {'x': x, 'src': src, 'dst': dst, 'edge_type_8': edge_type_8, 'L0_gnn_w1': _L0_gnn_in['w1'], 'L0_gnn_sl1': _L0_gnn_in['sl1'], 'L0_gnn_b1': _L0_gnn_in['b1'], 'L0_gnn_w2': _L0_gnn_in['w2'], 'L0_gnn_sl2': _L0_gnn_in['sl2'], 'L0_gnn_b2': _L0_gnn_in['b2'], 'L1_gnn_W1': _L1_gnn_in['W1'], 'L1_gnn_b1': _L1_gnn_in['b1'], 'L1_gnn_W2': _L1_gnn_in['W2'], 'L1_gnn_b2': _L1_gnn_in['b2']}

def reference(x, src, dst, edge_type_8, L0_gnn_w1, L0_gnn_sl1, L0_gnn_b1, L0_gnn_w2, L0_gnn_sl2, L0_gnn_b2, L1_gnn_W1, L1_gnn_b1, L1_gnn_W2, L1_gnn_b2):
    import jax
    import jax.numpy as jnp

    def _L0_gnn_ref(entity_emb, w1, sl1, b1, w2, sl2, b2, edge_index, edge_type):
        import jax, jax.numpy as jnp
        import numpy as np
        N_ENT = 12500

        def _rgcn_layer(x, W, SW, b, src, dst, rel):
            xt = jnp.einsum('nd,rde->rne', x, W)
            msg = xt[rel, src]
            agg = jax.ops.segment_sum(msg, dst, num_segments=x.shape[0])
            return jax.nn.relu(agg + x @ SW + b)
        src, dst = (edge_index[0], edge_index[1])
        x = _rgcn_layer(entity_emb, w1, sl1, b1, src, dst, edge_type)
        x = _rgcn_layer(x, w2, sl2, b2, src, dst, edge_type)
        return x

    def _L1_gnn_ref(x, src, dst, W1, b1, W2, b2):
        import jax, jax.numpy as jnp
        import numpy as np
        N_NODES = 12500
        N_EDGES = 400000
        D_IN = 128
        D_HID = 128
        D_OUT = 128
        N = x.shape[0]
        deg = jax.ops.segment_sum(jnp.ones_like(dst, dtype=jnp.float32), dst, num_segments=N)
        d_invsqrt = jnp.maximum(deg, 1.0) ** (-0.5)
        d_invsqrt = d_invsqrt[:, None]
        feat = jax.nn.relu(x @ W1 + b1)
        h = feat * d_invsqrt
        agg = jax.ops.segment_sum(h[src], dst, num_segments=N)
        feat = feat - agg * d_invsqrt
        return feat @ W2 + b2
    edge_index = jnp.stack([src, dst])
    x = _layernorm(x + _L0_gnn_ref(x, L0_gnn_w1, L0_gnn_sl1, L0_gnn_b1, L0_gnn_w2, L0_gnn_sl2, L0_gnn_b2, edge_index, edge_type_8), axis=-1)
    x = _layernorm(x + _L1_gnn_ref(x, src, dst, L1_gnn_W1, L1_gnn_b1, L1_gnn_W2, L1_gnn_b2), axis=-1)
    return x

_drawn_inputs = setup_inputs


def setup_inputs(seed=0):
    import zlib

    import numpy as np

    out = dict(_drawn_inputs(seed))
    spreads = {'L0_gnn_b1': (0.0, 0.1), 'L0_gnn_b2': (0.0, 0.8)}
    factors = {'L1_gnn_b1': 8.0, 'L1_gnn_b2': 5.92}
    for name, (base, spread) in spreads.items():
        noise = np.random.default_rng([zlib.crc32(name.encode()), seed]).standard_normal(out[name].shape)
        drawn = base * np.exp(spread * noise) if base else spread * noise
        out[name] = jnp.asarray(drawn.astype(out[name].dtype))
    for name, factor in factors.items():
        out[name] = (out[name] * factor).astype(out[name].dtype)
    return out
```

```python
import concourse.bass as bass
from concourse import mybir
from contextlib import ExitStack

F32 = mybir.dt.float32
I32 = mybir.dt.int32
BF16 = mybir.dt.bfloat16
ALU = mybir.AluOpType
ACT = mybir.ActivationFunctionType
AX = mybir.AxisListType

P = 128
D = 128
N = 12500
E = 212500
NREL = 8
EPS = 1e-5

KG = 7
GN = 64
TN = 16
TK = TN * NREL
HALVES = 2
UN = HALVES * KG
TB = 119
NTB = 14
NT = TB * NTB
NG = NT // KG
IT = NG // HALVES
assert NT * P >= E and IT * HALVES == NG and NT % KG == 0

CH = 512
CB = CH // P
NCH = -(-N // CH)
NPAIR = NCH // 2
NPAD = NCH * CH
LASTN = N - (NCH - 1) * CH
ACC = NPAD + GN


class Chain:

    def __init__(self, eng, sem, base):
        self.eng, self.sem, self.base, self.n = eng, sem, base, 0

    def then(self, ins):
        ins.then_inc(self.sem, 1)
        self.n += 1
        self.eng.wait_ge(self.sem, self.base + self.n)


def gate(eng, passed):
    eng.sem_inc(passed, 1)


def bc_last(ap, n):
    return ap.unsqueeze(len(ap.shape)).broadcast_to([*ap.shape, n])


def build(nc, x, src, dst, rel, w1, sl1, b1, w2, sl2, b2, gw1, gb1, gw2, gb2, out):
    top = ExitStack()
    with top:
        def sb(name, shape, dt=F32, ctx=top):
            return ctx.enter_context(nc.sbuf_tensor(name, shape, dt))

        tile_lo_d = nc.dram_tensor("tile_lo_d", (NT,), F32, kind="Internal").ap()
        tile_hi_d = nc.dram_tensor("tile_hi_d", (NT,), F32, kind="Internal").ap()
        x1_d = nc.dram_tensor("x1_d", (NPAD, D), F32, kind="Internal").ap()
        z_d = nc.dram_tensor("z_d", (NPAD, D), F32, kind="Internal").ap()
        feat_d = nc.dram_tensor("feat_d", (NPAD, D), F32, kind="Internal").ap()
        h_d = nc.dram_tensor("h_d", (NPAD, D), F32, kind="Internal").ap()

        W = [sb("w1s", [P, NREL, D]), sb("w2s", [P, NREL, D])]
        SL = [sb("sl1s", [P, D]), sb("sl2s", [P, D])]
        B = [sb("b1s", [P, 1]), sb("b2s", [P, 1])]
        GW1, GW2 = sb("gw1s", [P, D]), sb("gw2s", [P, D])
        GB1, GB2 = sb("gb1s", [P, D]), sb("gb2s", [P, D])
        ident = sb("ident", [P, P])
        iota = sb("iota", [P, TK])
        zeros_bf = sb("zeros_bf", [P, CH], BF16)
        ones_bf = sb("ones_bf", [P, 1], BF16)
        one = sb("one", [1, 1])
        eps = sb("eps", [P, 1])
        src_i = sb("src_i", [P, NT], I32)
        node = sb("node", [P, NT])
        relf = sb("relf", [P, NT])
        lo_b = sb("lo_b", [P, NT])
        glo = sb("glo", [P, NG])
        dinv = sb("dinv", [P, NPAD // P])
        acc = sb("acc", [P, ACC])
        rounds_i = sb("rounds_i", [1, 2], I32)

        passed = top.enter_context(nc.semaphore("passed"))
        psum = [top.enter_context(nc.psum_tensor(f"bank{i}", [P, CH], F32)) for i in range(8)]

        prologue(nc, top, x, src, dst, rel, w1, sl1, b1, w2, sl2, b2, gw1, gb1, gw2, gb2,
                 W, SL, B, GW1, GW2, GB1, GB2, ident, iota, zeros_bf, ones_bf, one, eps,
                 src_i, node, relf, lo_b, glo, rounds_i, tile_lo_d, tile_hi_d, psum)
        with ExitStack() as ctx:
            cnt = sb("cnt", [1, ACC], F32, ctx)
            relational_sum(nc, passed, "r1", x, W[0], src_i, node, relf, lo_b, glo, rounds_i, iota, zeros_bf, ones_bf,
                           acc, cnt, psum)
            dense1(nc, passed, x, x1_d, SL[0], B[0], ident, one, acc, cnt, dinv, psum)
        relational_sum(nc, passed, "r2", x1_d, W[1], src_i, node, relf, lo_b, glo, rounds_i, iota, zeros_bf, ones_bf,
                       acc, None, psum)
        dense2(nc, passed, x, x1_d, z_d, feat_d, h_d, SL[1], B[1], GW1, GB1, ident, eps, acc, dinv, psum)
        plain_sum(nc, passed, h_d, src_i, node, glo, rounds_i, iota, acc, psum)
        dense3(nc, passed, z_d, feat_d, out, GW2, GB2, ident, eps, acc, dinv, psum)


def prologue(nc, top, x, src, dst, rel, w1, sl1, b1, w2, sl2, b2, gw1, gb1, gw2, gb2,
             W, SL, B, GW1, GW2, GB1, GB2, ident, iota, zeros_bf, ones_bf, one, eps,
             src_i, node, relf, lo_b, glo, rounds_i, tile_lo_d, tile_hi_d, psum):
    with ExitStack() as ctx:
        def sb(name, shape, dt=F32):
            return ctx.enter_context(nc.sbuf_tensor(name, shape, dt))

        def sem(name):
            return ctx.enter_context(nc.semaphore(name))

        raw = [sb(f"raw{n}", [TB, NTB, P], I32) for n in ("d", "r", "s")]
        rawf = [sb(f"rawf{n}", [TB, NTB, P]) for n in ("d", "r", "s")]
        tlo, thi = sb("tlo", [TB, NTB]), sb("thi", [TB, NTB])
        hi_b = sb("hi_b", [P, NT])
        span = sb("span", [P, NT])
        ghi = sb("ghi", [P, NG])
        sp = sb("sp", [P, 8])
        spi = sb("spi", [P, 8], I32)
        padded, raw_in, consts, ident0 = sem("padded"), sem("raw_in"), sem("consts"), sem("ident0")
        weights_in, conv, turned, placed = sem("weights_in"), sem("conv"), sem("turned"), sem("placed")
        tile_out, tile_in, steps = sem("tile_out"), sem("tile_in"), sem("steps")
        block = ctx.enter_context(nc.Block())

        full = E // P
        before = (NTB - 1) * TB
        pads = (N, 0, 0)

        @block.sync
        def _(sync):
            sync.wait_ge(padded, 3)
            for a, r in zip((dst, rel, src), raw):
                sync.dma_start(r[:, 0:NTB - 1, :], a[0:before * P].rearrange("(j p e) -> p j e", j=NTB - 1, p=TB)
                               ).then_inc(raw_in, 16)
                sync.dma_start(r[0:full - before, NTB - 1, :],
                               a[before * P:full * P].rearrange("(p e) -> p e", e=P)).then_inc(raw_in, 16)
                sync.dma_start(r[full - before:full - before + 1, NTB - 1, 0:E - full * P],
                               a[full * P:E].rearrange("(p e) -> p e", p=1)).then_inc(raw_in, 16)
            loads = [(W[0], w1.rearrange("r i o -> i r o")), (W[1], w2.rearrange("r i o -> i r o")),
                     (SL[0], sl1), (SL[1], sl2), (GW1, gw1), (GW2, gw2),
                     (B[0], b1.rearrange("(p a) -> p a", a=1)), (B[1], b2.rearrange("(p a) -> p a", a=1)),
                     (GB1, gb1.partition_broadcast(P)), (GB2, gb2.partition_broadcast(P))]
            for to, of in loads:
                sync.dma_start(to[:], of).then_inc(weights_in, 16)
            sync.wait_ge(weights_in, 16 * len(loads))
            sync.wait_ge(conv, 5)
            sync.dma_start(tile_lo_d.rearrange("(j p) -> p j", p=TB), tlo[:, :],
                           allow_slow_non_contiguous=True).then_inc(tile_out, 16)
            sync.dma_start(tile_hi_d.rearrange("(j p) -> p j", p=TB), thi[:, :],
                           allow_slow_non_contiguous=True).then_inc(tile_out, 16)
            sync.wait_ge(tile_out, 32)
            sync.dma_start(lo_b[:, :], tile_lo_d.partition_broadcast(P)).then_inc(tile_in, 16)
            sync.dma_start(hi_b[:, :], tile_hi_d.partition_broadcast(P)).then_inc(tile_in, 16)

        @block.gpsimd
        def _(pool):
            nc.gpsimd.memset(ident[:, :], 0.0).then_inc(ident0, 1)
            pool.wait_ge(ident0, 1)
            nc.gpsimd.affine_select(out=ident[:, :], in_=ident[:, :], compare_op=ALU.not_equal, fill=1.0, base=0,
                                    pattern=[[-1, P]], channel_multiplier=1).then_inc(consts, 1)
            nc.gpsimd.iota(iota[:, :], [[1, TK]], base=0, channel_multiplier=0,
                           allow_small_or_imprecise_dtypes=True).then_inc(consts, 1)

        @block.vector
        def _(dve):
            for r, pad in zip(raw, pads):
                dve.memset(r[:, NTB - 1, :], pad).then_inc(padded, 1)
            dve.memset(zeros_bf[:, :], 0.0).then_inc(consts, 1)
            dve.memset(ones_bf[:, :], 1.0).then_inc(consts, 1)
            dve.memset(one[:, :], 1.0).then_inc(consts, 1)
            dve.memset(eps[:, :], EPS).then_inc(consts, 1)
            dve.wait_ge(raw_in, 16 * 9)
            for r, f in zip(raw, rawf):
                dve.tensor_copy(f[:, :, :], r[:, :, :]).then_inc(conv, 1)
            dve.wait_ge(conv, 3)
            dve.tensor_reduce(tlo[:, :], rawf[0][:, :, :], AX.X, ALU.min).then_inc(conv, 1)
            dve.tensor_reduce(thi[:, :], rawf[0][:, :, :], AX.X, ALU.max).then_inc(conv, 1)
            for b, (to, j0) in enumerate(banks_of((node, relf, src_i))):
                n = min(4, NTB - j0) * TB
                dve.wait_ge(turned, b + 1)
                dve.tensor_copy(to[:, j0 * TB:j0 * TB + n], psum[b % 8][:, 0:n]).then_inc(placed, 1)
            dve.wait_ge(tile_in, 32)
            ch = Chain(dve, steps, 0)
            ch.then(dve.tensor_reduce(glo[:, :], lo_b[:, :].rearrange("p (g k) -> p g k", k=KG), AX.X, ALU.min))
            ch.then(dve.tensor_reduce(ghi[:, :], hi_b[:, :].rearrange("p (g k) -> p g k", k=KG), AX.X, ALU.max))
            ch.then(dve.tensor_tensor(span[:, :], hi_b[:, :], lo_b[:, :], ALU.subtract))
            ch.then(dve.tensor_reduce(sp[:, 0:1], span[:, :], AX.X, ALU.max))
            ch.then(dve.tensor_tensor(ghi[:, :], ghi[:, :], glo[:, :], ALU.subtract))
            ch.then(dve.tensor_reduce(sp[:, 1:2], ghi[:, :], AX.X, ALU.max))
            ch.then(dve.tensor_copy(spi[:, 0:1], sp[:, 1:2]))
            ch.then(dve.tensor_scalar(spi[:, 1:2], spi[:, 0:1], 6, None, ALU.arith_shift_right))
            ch.then(dve.tensor_copy(sp[:, 2:3], spi[:, 1:2]))
            ch.then(dve.tensor_scalar(sp[:, 3:4], sp[:, 2:3], 1.0, None, ALU.add))
            ch.then(dve.tensor_scalar(sp[:, 4:5], sp[:, 0:1], float(TN), None, ALU.is_ge))
            ch.then(dve.tensor_scalar(sp[:, 5:6], sp[:, 1:2], float(GN), None, ALU.is_ge))
            ch.then(dve.tensor_tensor(sp[:, 4:5], sp[:, 4:5], sp[:, 5:6], ALU.max))
            ch.then(dve.tensor_scalar(sp[:, 5:6], sp[:, 3:4], float(GN // TN), -1.0, ALU.mult, ALU.add))
            ch.then(dve.tensor_tensor(sp[:, 5:6], sp[:, 5:6], sp[:, 4:5], ALU.mult))
            ch.then(dve.tensor_scalar(sp[:, 2:3], sp[:, 5:6], 1.0, None, ALU.add))
            ch.then(dve.tensor_copy(rounds_i[:, :], sp[0:1, 2:4]))

        @block.tensor
        def _(pe):
            pe.wait_ge(conv, 3)
            pe.wait_ge(consts, 6)
            b = 0
            for n, (to, j0) in enumerate(banks_of((0, 1, 2))):
                if n >= 8:
                    pe.wait_ge(placed, n - 7)
                for j in range(j0, min(j0 + 4, NTB)):
                    mm = pe.transpose(psum[n % 8][:, (j - j0) * TB:(j - j0 + 1) * TB], rawf[to][:, j, :],
                                      ident[0:TB, 0:TB])
                mm.then_inc(turned, 1)


def banks_of(tensors):
    return [(t, j0) for t in tensors for j0 in range(0, NTB, 4)]


def gather_sems(sem, tag):
    return [[sem(f"{tag}_landed{h}_{k}") for k in range(KG)] for h in range(HALVES)]


def relational_sum(nc, passed, tag, table, W, src_i, node, relf, lo_b, glo, rounds_i, iota, zeros_bf, ones_bf,
                   acc, cnt, psum):
    with ExitStack() as ctx:
        def sb(name, shape, dt=F32):
            return ctx.enter_context(nc.sbuf_tensor(f"{tag}_{name}", shape, dt))

        def sem(name):
            return ctx.enter_context(nc.semaphore(f"{tag}_{name}"))

        G = sb("G", [P, UN, D])
        idx = sb("idx", [P, UN], I32)
        S = sb("S", [P, UN, TK])
        agg = sb("agg", [P, HALVES, GN, NREL])
        key = sb("key", [P, NT])
        t1, t2, t3 = sb("t1", [P, NT]), sb("t2", [P, NT]), sb("t3", [P, NT])
        gs = sb("gs", [P, NG])
        step_t, step_g = sb("step_t", [P, 1]), sb("step_g", [P, 1])
        carry = sb("carry", [P, 1])
        off_i = sb("off_i", [1, NG, 8], I32)
        gs_i = sb("gs_i", [1, NG], I32)
        dsum = sb("dsum", [1, HALVES, GN])

        landed = gather_sems(sem, "g")
        idx_ready = [sem(f"idx_ready{h}") for h in range(HALVES)]
        hot_ready = [sem(f"hot_ready{h}") for h in range(HALVES)]
        summed = [sem(f"summed{h}") for h in range(HALVES)]
        agg_out = [sem(f"agg_out{h}") for h in range(HALVES)]
        mixed = [sem(f"mixed{h}") for h in range(HALVES)]
        added = [sem(f"added{h}") for h in range(HALVES)]
        tables, steps, setup = sem("tables"), sem("steps"), sem("setup")
        block = ctx.enter_context(nc.Block())

        agg_ps, mix_ps, cnt_ps = psum[0:2], psum[2:4], psum[4:6]

        def rounds_of(eng):
            return eng.value_load(rounds_i[0:1, 0:1], min_val=1, max_val=4 * (N // GN + 1))

        def take(act, h, i, n):
            act.wait_ge(summed[h], n + 1)
            act.copy(idx[:, h * KG:(h + 1) * KG], src_i[:, bass.ds(i * UN + h * KG, KG)]).then_inc(idx_ready[h], 1)

        def copy_out(act, h, n):
            act.wait_ge(summed[h], n + 2)
            act.wait_ge(mixed[h], n + 1)
            act.copy(agg[:, h, :, :], agg_ps[h][:, :].rearrange("p (n r) -> p n r", r=NREL)).then_inc(agg_out[h], 1)

        @block.scalar
        def _(act):
            rounds = rounds_of(act)
            with act.Fori(0, rounds) as q:
                first = act.snap(q * IT)
                for h in range(HALVES):
                    take(act, h, 0, first)
                with act.Fori(0, IT - 1) as i:
                    n = act.snap(q * IT + i)
                    for h in range(HALVES):
                        copy_out(act, h, n)
                        take(act, h, i + 1, n + 1)
                last = act.snap(q * IT + (IT - 1))
                for h in range(HALVES):
                    copy_out(act, h, last)

        @block.gpsimd
        def _(pool):
            rounds = rounds_of(pool)
            with pool.Fori(0, rounds) as q:
                with pool.Fori(0, IT) as i:
                    n = pool.snap(q * IT + i)
                    for h in range(HALVES):
                        pool.wait_ge(idx_ready[h], n + 1)
                        pool.wait_ge(summed[h], n + 1)
                        gate(pool, passed)
                        for k in range(KG):
                            s = h * KG + k
                            pool.indirect_dma_start(
                                out=G[:, s, :], out_offset=None, in_=table[:, :],
                                in_offset=bass.IndirectOffsetOnAxis(ap=idx[:, s:s + 1], axis=0)
                            ).then_inc(landed[h][k], 16)

        @block.tensor
        def _(pe):
            for h in range(HALVES):
                pe.sem_inc(summed[h], 1)
                pe.sem_inc(mixed[h], 1)
            rounds = rounds_of(pe)
            with pe.Fori(0, rounds) as q:
                pe.wait_ge(tables, q + 1)
                gate(pe, passed)
                with pe.Fori(0, IT) as i:
                    n = pe.snap(q * IT + i)
                    for h in range(HALVES):
                        _, offs = nc.values_load_multi_w_load_instructions(
                            off_i[0:1, bass.ds(i * HALVES + h, 1), 0:KG], engines=bass.OrderedEngineSet([pe.engine]),
                            min_val=0, max_val=(GN - TN) * NREL, skip_runtime_bounds_check_because="clamped on the chip")
                        pe.wait_ge(agg_out[h], n + 1)
                        pe.matmul(agg_ps[h][:, :], zeros_bf[:, 0:P], zeros_bf[:, :], start=True, stop=False,
                                  skip_group_check=True)
                        if cnt is not None:
                            pe.wait_ge(added[h], n + 1)
                            pe.matmul(cnt_ps[h][0:1, :], zeros_bf[:, 0:1], zeros_bf[:, :], start=True, stop=False,
                                      skip_group_check=True)
                        pe.wait_ge(hot_ready[h], n + 1)
                        for k in range(KG):
                            s = h * KG + k
                            pe.wait_ge(landed[h][k], 16 * n + 16)
                            mm = pe.matmul(agg_ps[h][:, bass.ds(offs[k], TK)], G[:, s, :], S[:, s, :],
                                           start=False, stop=(k == KG - 1), skip_group_check=True)
                            if cnt is not None:
                                mm = pe.matmul(cnt_ps[h][0:1, bass.ds(offs[k], TK)], ones_bf[:, :],
                                               S[:, s, :].bitcast(BF16)[:, 1:2 * TK:2],
                                               start=False, stop=(k == KG - 1), skip_group_check=True)
                        mm.then_inc(summed[h], 1)
                    for h in range(HALVES):
                        pe.wait_ge(agg_out[h], n + 2)
                        pe.wait_ge(added[h], n + 1)
                        for r in range(NREL):
                            mm = pe.matmul(mix_ps[h][:, 0:GN], W[:, r, :], agg[:, h, :, r],
                                           start=(r == 0), stop=(r == NREL - 1))
                        mm.then_inc(mixed[h], 1)

        @block.vector
        def _(dve):
            dve.memset(acc[:, :], 0.0).then_inc(setup, 1)
            dve.memset(step_t[:, :], 0.0).then_inc(setup, 1)
            dve.memset(step_g[:, :], 0.0).then_inc(setup, 1)
            if cnt is not None:
                dve.memset(cnt[:, :], 0.0).then_inc(setup, 1)
            dve.wait_ge(setup, 3 if cnt is None else 4)
            for h in range(HALVES):
                dve.sem_inc(added[h], 1)
                dve.sem_inc(agg_out[h], 1)
            rounds = rounds_of(dve)
            per_table = 20
            per_iter = HALVES * (1 if cnt is None else 3)
            per_round = per_table + IT * per_iter
            by_group = lambda a: a[:, :].rearrange("p (g k) -> p g k", k=KG)
            with dve.Fori(0, rounds) as q:
                ch = Chain(dve, steps, q * per_round)
                gsb = bc_last(gs[:, :], KG)
                ch.then(dve.tensor_scalar(gs[:, :], glo[:, :], step_g[:, 0:1], None, ALU.add))
                ch.then(dve.tensor_tensor(by_group(t1), by_group(lo_b), gsb, ALU.max))
                ch.then(dve.tensor_scalar(t1[:, :], t1[:, :], step_t[:, 0:1], None, ALU.add))
                ch.then(dve.scalar_tensor_tensor(by_group(t2), gsb, float(GN - TN), by_group(t1), ALU.add, ALU.min))
                ch.then(dve.tensor_tensor(by_group(t3), by_group(t2), gsb, ALU.subtract))
                ch.then(dve.tensor_scalar(off_i[0:1, :, 0:KG], by_group(t3)[0:1, :, :], float(NREL), None, ALU.mult))
                ch.then(dve.tensor_scalar(gs_i[:, :], gs[0:1, :], float(NPAD), None, ALU.min))
                ch.then(dve.tensor_tensor(t1[:, :], node[:, :], t1[:, :], ALU.subtract))
                ch.then(dve.tensor_scalar(t3[:, :], t1[:, :], 0.0, None, ALU.is_ge))
                ch.then(dve.scalar_tensor_tensor(t3[:, :], t1[:, :], float(TN), t3[:, :], ALU.is_lt, ALU.mult))
                ch.then(dve.tensor_tensor(by_group(t1), by_group(node), gsb, ALU.subtract))
                ch.then(dve.scalar_tensor_tensor(t3[:, :], t1[:, :], float(GN), t3[:, :], ALU.is_lt, ALU.mult))
                ch.then(dve.tensor_tensor(t1[:, :], node[:, :], t2[:, :], ALU.subtract))
                ch.then(dve.scalar_tensor_tensor(t1[:, :], t1[:, :], float(NREL), relf[:, :], ALU.mult, ALU.add))
                ch.then(dve.scalar_tensor_tensor(t1[:, :], t1[:, :], 1.0, t3[:, :], ALU.add, ALU.mult))
                ch.then(dve.tensor_scalar(key[:, :], t1[:, :], -1.0, None, ALU.add))
                ch.then(dve.tensor_scalar(step_t[:, :], step_t[:, :], float(TN), None, ALU.add))
                ch.then(dve.tensor_scalar(carry[:, :], step_t[:, :], float(GN), float(GN), ALU.is_ge, ALU.mult))
                ch.then(dve.tensor_tensor(step_t[:, :], step_t[:, :], carry[:, :], ALU.subtract))
                ch.then(dve.tensor_tensor(step_g[:, :], step_g[:, :], carry[:, :], ALU.add))
                assert ch.n == per_table
                dve.sem_inc(tables, 1)
                with dve.Fori(0, IT) as i:
                    n = dve.snap(q * IT + i)
                    ch = Chain(dve, steps, dve.snap(q * per_round + i * per_iter + per_table))
                    for h in range(HALVES):
                        s = h * KG
                        dve.wait_ge(summed[h], n + 1)
                        dve.tensor_tensor(
                            S[:, s:s + KG, :], iota[:, :].unsqueeze(1).broadcast_to([P, KG, TK]),
                            bc_last(key[:, bass.ds(i * UN + s, KG)], TK), ALU.is_equal).then_inc(hot_ready[h], 1)
                    for h in range(HALVES):
                        g0 = dve.value_load(gs_i[0:1, bass.ds(i * HALVES + h, 1)], min_val=0, max_val=NPAD)
                        if cnt is not None:
                            dve.wait_ge(summed[h], n + 2)
                            ch.then(dve.tensor_reduce(dsum[:, h, :],
                                                      cnt_ps[h][0:1, :].rearrange("p (n r) -> p n r", r=NREL),
                                                      AX.X, ALU.add))
                            window = cnt[:, bass.ds(g0, GN)]
                            ch.then(dve.tensor_tensor(window, window, dsum[:, h, :], ALU.add))
                        dve.wait_ge(mixed[h], n + 2)
                        window = acc[:, bass.ds(g0, GN)]
                        ins = dve.tensor_tensor(window, window, mix_ps[h][:, 0:GN], ALU.add)
                        ch.then(ins)
                        dve.sem_inc(added[h], 1)
                    assert ch.n == per_iter


def plain_sum(nc, passed, table, src_i, node, glo, rounds_i, iota, acc, psum):
    tag = "r3"
    with ExitStack() as ctx:
        def sb(name, shape, dt=F32):
            return ctx.enter_context(nc.sbuf_tensor(f"{tag}_{name}", shape, dt))

        def sem(name):
            return ctx.enter_context(nc.semaphore(f"{tag}_{name}"))

        G = sb("G", [P, UN, D])
        idx = sb("idx", [P, UN], I32)
        S = sb("S", [P, UN, GN])
        key = sb("key", [P, NT])
        gs = sb("gs", [P, NG])
        step_g = sb("step_g", [P, 1])
        gs_i = sb("gs_i", [1, NG], I32)
        landed = gather_sems(sem, "g")
        idx_ready = [sem(f"idx_ready{h}") for h in range(HALVES)]
        hot_ready = [sem(f"hot_ready{h}") for h in range(HALVES)]
        summed = [sem(f"summed{h}") for h in range(HALVES)]
        added = [sem(f"added{h}") for h in range(HALVES)]
        steps, setup = sem("steps"), sem("setup")
        block = ctx.enter_context(nc.Block())
        sum_ps = psum[0:2]

        def rounds_of(eng):
            return eng.value_load(rounds_i[0:1, 1:2], min_val=1, max_val=N // GN + 1)

        def take(act, h, i, n):
            act.wait_ge(summed[h], n + 1)
            act.copy(idx[:, h * KG:(h + 1) * KG], src_i[:, bass.ds(i * UN + h * KG, KG)]).then_inc(idx_ready[h], 1)

        @block.scalar
        def _(act):
            rounds = rounds_of(act)
            with act.Fori(0, rounds) as q:
                first = act.snap(q * IT)
                for h in range(HALVES):
                    take(act, h, 0, first)
                with act.Fori(1, IT) as i:
                    n = act.snap(q * IT + i)
                    for h in range(HALVES):
                        take(act, h, i, n)

        @block.gpsimd
        def _(pool):
            rounds = rounds_of(pool)
            with pool.Fori(0, rounds) as q:
                with pool.Fori(0, IT) as i:
                    n = pool.snap(q * IT + i)
                    for h in range(HALVES):
                        pool.wait_ge(idx_ready[h], n + 1)
                        pool.wait_ge(summed[h], n + 1)
                        gate(pool, passed)
                        for k in range(KG):
                            s = h * KG + k
                            pool.indirect_dma_start(
                                out=G[:, s, :], out_offset=None, in_=table[:, :],
                                in_offset=bass.IndirectOffsetOnAxis(ap=idx[:, s:s + 1], axis=0)
                            ).then_inc(landed[h][k], 16)

        @block.tensor
        def _(pe):
            for h in range(HALVES):
                pe.sem_inc(summed[h], 1)
            rounds = rounds_of(pe)
            with pe.Fori(0, rounds) as q:
                with pe.Fori(0, IT) as i:
                    n = pe.snap(q * IT + i)
                    for h in range(HALVES):
                        pe.wait_ge(added[h], n + 1)
                        pe.wait_ge(hot_ready[h], n + 1)
                        for k in range(KG):
                            s = h * KG + k
                            pe.wait_ge(landed[h][k], 16 * n + 16)
                            mm = pe.matmul(sum_ps[h][:, 0:GN], G[:, s, :], S[:, s, :], start=(k == 0),
                                           stop=(k == KG - 1))
                        mm.then_inc(summed[h], 1)

        @block.vector
        def _(dve):
            dve.memset(acc[:, :], 0.0).then_inc(setup, 1)
            dve.memset(step_g[:, :], 0.0).then_inc(setup, 1)
            dve.wait_ge(setup, 2)
            for h in range(HALVES):
                dve.sem_inc(added[h], 1)
            rounds = rounds_of(dve)
            per_table, per_iter = 4, HALVES
            per_round = per_table + IT * per_iter
            with dve.Fori(0, rounds) as q:
                ch = Chain(dve, steps, q * per_round)
                ch.then(dve.tensor_scalar(gs[:, :], glo[:, :], step_g[:, 0:1], None, ALU.add))
                ch.then(dve.tensor_scalar(gs_i[:, :], gs[0:1, :], float(NPAD), None, ALU.min))
                ch.then(dve.tensor_tensor(key[:, :].rearrange("p (g k) -> p g k", k=KG),
                                          node[:, :].rearrange("p (g k) -> p g k", k=KG), bc_last(gs[:, :], KG),
                                          ALU.subtract))
                ch.then(dve.tensor_scalar(step_g[:, :], step_g[:, :], float(GN), None, ALU.add))
                assert ch.n == per_table
                gate(dve, passed)
                with dve.Fori(0, IT) as i:
                    n = dve.snap(q * IT + i)
                    ch = Chain(dve, steps, dve.snap(q * per_round + i * per_iter + per_table))
                    for h in range(HALVES):
                        s = h * KG
                        dve.wait_ge(summed[h], n + 1)
                        dve.tensor_tensor(
                            S[:, s:s + KG, :], iota[:, 0:GN].unsqueeze(1).broadcast_to([P, KG, GN]),
                            bc_last(key[:, bass.ds(i * UN + s, KG)], GN), ALU.is_equal).then_inc(hot_ready[h], 1)
                    for h in range(HALVES):
                        g0 = dve.value_load(gs_i[0:1, bass.ds(i * HALVES + h, 1)], min_val=0, max_val=NPAD)
                        dve.wait_ge(summed[h], n + 2)
                        window = acc[:, bass.ds(g0, GN)]
                        ch.then(dve.tensor_tensor(window, window, sum_ps[h][:, 0:GN], ALU.add))
                        dve.sem_inc(added[h], 1)
                    assert ch.n == per_iter


def pairs(eng, body):
    body(0, [(0, 0, False), (1, 1, False)])
    with eng.Fori(1, NPAIR) as i:
        body(i, [(0, eng.snap(i * 2), False), (1, eng.snap(i * 2 + 1), False)])
    body(NPAIR, [(0, NCH - 1, True)])


def stored(eng, sem, i, n):
    if not (isinstance(i, int) and i == 0):
        eng.wait_ge(sem, i * (16 * n))


def rows(table, c):
    return table[bass.ds(c * CH, CH), :].rearrange("(a p) f -> p a f", p=P)


def load_rows(eng, to, table, c, last, padded_table, landed):
    if last and not padded_table:
        whole, part = divmod(LASTN, P)
        assert whole == 1
        eng.dma_start(to[:, 0, :], table[N - LASTN:N - part, :]).then_inc(landed, 16)
        eng.dma_start(to[0:part, 1, :], table[N - part:N, :]).then_inc(landed, 16)
    else:
        for a in range(2):
            eng.dma_start(to[:, 2 * a:2 * a + 2, :], rows(table, c)[:, 2 * a:2 * a + 2, :]).then_inc(landed, 16)


def dense1(nc, passed, x, x1_d, SL, B, ident, one, acc, cnt, dinv, psum):
    with ExitStack() as ctx:
        def sb(name, shape, dt=F32):
            return ctx.enter_context(nc.sbuf_tensor(f"d1_{name}", shape, dt))

        def sem(name):
            return ctx.enter_context(nc.semaphore(f"d1_{name}"))

        xr, xT = sb("xr", [P, 2, CB, D]), sb("xT", [P, 2, CH])
        pre, yT, yr = sb("pre", [P, 2, CH]), sb("yT", [P, 2, CH]), sb("yr", [P, 2, CB, D])
        deg = sb("deg", [P, 2, NPAD // P])
        x_in, y_out = [sem(f"x_in{u}") for u in range(2)], [sem(f"y_out{u}") for u in range(2)]
        x_turned, xT_done, selfed, pre_done, act_done, y_turned, y_done = (
            sem(n) for n in ("x_turned", "xT_done", "selfed", "pre_done", "act_done", "y_turned", "y_done"))
        counts, degs, padded = sem("counts"), sem("degs"), sem("padded")
        block = ctx.enter_context(nc.Block())
        PT, PS, PO, PD = psum[0:2], psum[2:4], psum[4:6], psum[6]

        @block.sync
        def _(sync):
            def body(i, chunks):
                for u, c, last in chunks:
                    sync.wait_ge(x_turned, c + 1)
                    if last:
                        sync.wait_ge(padded, 1)
                    load_rows(sync, xr[:, u], x, c, last, False, x_in[u])
            pairs(sync, body)

        @block.tensor
        def _(pe):
            pe.sem_inc(x_turned, 2)
            pe.sem_inc(selfed, 2)
            pe.sem_inc(y_turned, 2)
            for b in range(NPAD // P):
                mm = pe.matmul(PD[:, b:b + 1], cnt[0:1, b * P:(b + 1) * P], one[:, :], start=True, stop=True)
            mm.then_inc(counts, 1)

            def body(i, chunks):
                for u, c, last in chunks:
                    pe.wait_ge(x_in[u], 32 * i + 32)
                    pe.wait_ge(xT_done, c + 1)
                    for a in range(CB):
                        mm = pe.transpose(PT[u][:, a * P:(a + 1) * P], xr[:, u, a, :], ident[:, :])
                    mm.then_inc(x_turned, 1)
                for u, c, last in chunks:
                    pe.wait_ge(xT_done, c + 3)
                    pe.wait_ge(pre_done, c + 1)
                    pe.matmul(PS[u][:, :], SL[:, :], xT[:, u, :], start=True, stop=True).then_inc(selfed, 1)
                for u, c, last in chunks:
                    pe.wait_ge(act_done, c + 3)
                    pe.wait_ge(y_done, c + 1)
                    for a in range(CB):
                        mm = pe.transpose(PO[u][:, a * P:(a + 1) * P], yT[:, u, a * P:(a + 1) * P], ident[:, :])
                    mm.then_inc(y_turned, 1)
            pairs(pe, body)

        @block.scalar
        def _(act):
            act.sem_inc(xT_done, 2)
            act.sem_inc(act_done, 2)
            act.wait_ge(degs, 1)
            act.activation(deg[:, 1, :], deg[:, 0, :], ACT.Sqrt).then_inc(degs, 1)

            def body(i, chunks):
                for u, c, last in chunks:
                    act.wait_ge(x_turned, c + 3)
                    act.wait_ge(selfed, c + 1)
                    act.copy(xT[:, u, :], PT[u][:, :]).then_inc(xT_done, 1)
                for u, c, last in chunks:
                    act.wait_ge(pre_done, c + 3)
                    act.wait_ge(y_turned, c + 1)
                    act.activation(yT[:, u, :], pre[:, u, :], ACT.Relu, bias=B[:, 0:1]).then_inc(act_done, 1)
            pairs(act, body)

        @block.vector
        def _(dve):
            dve.sem_inc(pre_done, 2)
            dve.sem_inc(y_done, 2)
            dve.wait_ge(counts, 1)
            dve.tensor_scalar(deg[:, 0, :], PD[:, 0:NPAD // P], 1.0, None, ALU.max).then_inc(degs, 1)
            dve.wait_ge(degs, 2)
            dve.reciprocal(dinv[:, :], deg[:, 1, :]).then_inc(degs, 1)

            def body(i, chunks):
                for u, c, last in chunks:
                    if last:
                        dve.wait_ge(x_turned, c + 1)
                        dve.memset(xr[:, u, :, :], 0.0).then_inc(padded, 1)
                    dve.wait_ge(selfed, c + 3)
                    dve.wait_ge(act_done, c + 1)
                    dve.tensor_tensor(pre[:, u, :], PS[u][:, :], acc[:, bass.ds(c * CH, CH)], ALU.add
                                      ).then_inc(pre_done, 1)
                for u, c, last in chunks:
                    dve.wait_ge(y_turned, c + 3)
                    stored(dve, y_out[u], i, 1)
                    dve.tensor_copy(yr[:, u, :, :], PO[u][:, :].rearrange("p (a f) -> p a f", a=CB)).then_inc(y_done, 1)
            pairs(dve, body)

        @block.gpsimd
        def _(pool):
            def body(i, chunks):
                for u, c, last in chunks:
                    pool.wait_ge(y_done, c + 3)
                    gate(pool, passed)
                    pool.dma_start(rows(x1_d, c), yr[:, u, :, :]).then_inc(y_out[u], 16)
            pairs(pool, body)
            pool.wait_ge(y_out[0], 16 * (NPAIR + 1))
            pool.wait_ge(y_out[1], 16 * NPAIR)


def dense2(nc, passed, x, x1_d, z_d, feat_d, h_d, SL, B, GW1, GB1, ident, eps, acc, dinv, psum):
    with ExitStack() as ctx:
        def sb(name, shape, dt=F32):
            return ctx.enter_context(nc.sbuf_tensor(f"d2_{name}", shape, dt))

        def sem(name):
            return ctx.enter_context(nc.semaphore(f"d2_{name}"))

        x1r, xr = sb("x1r", [P, 2, CB, D]), sb("xr", [P, 2, CB, D])
        xT, pre, yT = sb("xT", [P, 2, CH]), sb("pre", [P, 2, CH]), sb("yT", [P, 2, CH])
        rr, zr, zT = sb("rr", [P, 2, CB, D]), sb("zr", [P, 2, CB, D]), sb("zT", [P, 2, CH])
        fp, fr, hr = sb("fp", [P, 2, CB, D]), sb("fr", [P, 2, CB, D]), sb("hr", [P, 2, CB, D])
        st, mv, sd = sb("st", [P, 2, CB, 6]), sb("mv", [P, 2, CB, 2]), sb("sd", [P, 2, 2, CB])
        x_in = [sem(f"x_in{u}") for u in range(2)]
        z_out, f_out, h_out = ([sem(f"{n}_out{u}") for u in range(2)] for n in "zfh")
        (x_turned, xT_done, selfed, pre_done, y_act, y_turned, res_done, var_done, sd_done, z_done, z_turned, zT_done,
         f_mm, f_pre, f_done, h_done, padded, steps) = (
            sem(n) for n in ("x_turned", "xT_done", "selfed", "pre_done", "y_act", "y_turned", "res_done", "var_done",
                             "sd_done", "z_done", "z_turned", "zT_done", "f_mm", "f_pre", "f_done", "h_done", "padded",
                             "steps"))
        block = ctx.enter_context(nc.Block())
        PT, PS, PO = psum[0:2], psum[2:4], psum[4:6]
        PZ = PT
        PF = PS

        @block.sync
        def _(sync):
            def body(i, chunks):
                for u, c, last in chunks:
                    sync.wait_ge(x_turned, c + 1)
                    sync.wait_ge(res_done, c + 1)
                    if last:
                        sync.wait_ge(padded, 1)
                    load_rows(sync, x1r[:, u], x1_d, c, last, True, x_in[u])
                    load_rows(sync, xr[:, u], x, c, last, False, x_in[u])
            pairs(sync, body)

        @block.tensor
        def _(pe):
            for s in (x_turned, selfed, y_turned, z_turned, f_mm):
                pe.sem_inc(s, 2)

            def body(i, chunks):
                for u, c, last in chunks:
                    pe.wait_ge(x_in[u], 64 * i + 64)
                    pe.wait_ge(zT_done, c + 1)
                    for a in range(CB):
                        mm = pe.transpose(PT[u][:, a * P:(a + 1) * P], x1r[:, u, a, :], ident[:, :])
                    mm.then_inc(x_turned, 1)
                for u, c, last in chunks:
                    pe.wait_ge(xT_done, c + 3)
                    pe.wait_ge(f_pre, c + 1)
                    pe.matmul(PS[u][:, :], SL[:, :], xT[:, u, :], start=True, stop=True).then_inc(selfed, 1)
                for u, c, last in chunks:
                    pe.wait_ge(y_act, c + 3)
                    pe.wait_ge(res_done, c + 1)
                    for a in range(CB):
                        mm = pe.transpose(PO[u][:, a * P:(a + 1) * P], yT[:, u, a * P:(a + 1) * P], ident[:, :])
                    mm.then_inc(y_turned, 1)
                for u, c, last in chunks:
                    pe.wait_ge(z_done, c + 3)
                    pe.wait_ge(xT_done, c + 3)
                    for a in range(CB):
                        mm = pe.transpose(PZ[u][:, a * P:(a + 1) * P], zr[:, u, a, :], ident[:, :])
                    mm.then_inc(z_turned, 1)
                for u, c, last in chunks:
                    pe.wait_ge(zT_done, c + 3)
                    pe.wait_ge(pre_done, c + 3)
                    for a in range(CB):
                        mm = pe.matmul(PF[u][:, a * D:(a + 1) * D], zT[:, u, a * P:(a + 1) * P], GW1[:, :],
                                       start=True, stop=True)
                    mm.then_inc(f_mm, 1)
            pairs(pe, body)

        @block.scalar
        def _(act):
            for s in (xT_done, y_act, zT_done, f_done):
                act.sem_inc(s, 2)

            def body(i, chunks):
                for u, c, last in chunks:
                    act.wait_ge(x_turned, c + 3)
                    act.wait_ge(selfed, c + 1)
                    act.copy(xT[:, u, :], PT[u][:, :]).then_inc(xT_done, 1)
                for u, c, last in chunks:
                    act.wait_ge(pre_done, c + 3)
                    act.wait_ge(y_turned, c + 1)
                    act.activation(yT[:, u, :], pre[:, u, :], ACT.Relu, bias=B[:, 0:1]).then_inc(y_act, 1)
                for u, c, last in chunks:
                    act.wait_ge(var_done, c + 1)
                    act.activation(sd[:, u, 0, :], mv[:, u, :, 1], ACT.Sqrt, bias=eps[:, 0:1]).then_inc(sd_done, 1)
                for u, c, last in chunks:
                    act.wait_ge(z_turned, c + 3)
                    act.wait_ge(f_mm, c + 1)
                    act.copy(zT[:, u, :], PZ[u][:, :]).then_inc(zT_done, 1)
                for u, c, last in chunks:
                    act.wait_ge(f_pre, c + 3)
                    stored(act, f_out[u], i, 1)
                    act.wait_ge(h_done, c + 1)
                    act.activation(fr[:, u, :, :], fp[:, u, :, :], ACT.Relu).then_inc(f_done, 1)
            pairs(act, body)

        @block.vector
        def _(dve):
            for s in (pre_done, res_done, z_done, f_pre, h_done):
                dve.sem_inc(s, 2)
            b1b = GB1[:, :].unsqueeze(1).broadcast_to([P, CB, D])

            def body(i, chunks):
                ch = Chain(dve, steps, i * (2 * 4))
                for u, c, last in chunks:
                    if last:
                        dve.wait_ge(res_done, c + 1)
                        dve.memset(xr[:, u, :, :], 0.0).then_inc(padded, 1)
                    dve.wait_ge(selfed, c + 3)
                    dve.wait_ge(y_act, c + 1)
                    dve.tensor_tensor(pre[:, u, :], PS[u][:, :], acc[:, bass.ds(c * CH, CH)], ALU.add
                                      ).then_inc(pre_done, 1)
                for u, c, last in chunks:
                    dve.wait_ge(y_turned, c + 3)
                    dve.wait_ge(x_in[u], 64 * i + 64)
                    dve.tensor_tensor(rr[:, u, :, :], PO[u][:, :].rearrange("p (a f) -> p a f", a=CB), xr[:, u, :, :],
                                      ALU.add).then_inc(res_done, 1)
                    dve.wait_ge(res_done, c + 3)
                    stats(dve, ch, passed, rr[:, u], st[:, u], mv[:, u])
                    dve.sem_inc(var_done, 1)
                for u, c, last in chunks:
                    dve.wait_ge(sd_done, c + 1)
                    ch.then(dve.reciprocal(sd[:, u, 1, :], sd[:, u, 0, :]))
                    stored(dve, z_out[u], i, 1)
                    dve.wait_ge(z_turned, c + 1)
                    normed(dve, ch, rr[:, u], mv[:, u], sd[:, u, 1], zr[:, u])
                    dve.sem_inc(z_done, 1)
                for u, c, last in chunks:
                    dve.wait_ge(f_mm, c + 3)
                    dve.wait_ge(f_done, c + 1)
                    dve.tensor_tensor(fp[:, u, :, :], PF[u][:, :].rearrange("p (a f) -> p a f", a=CB), b1b, ALU.add
                                      ).then_inc(f_pre, 1)
                for u, c, last in chunks:
                    dve.wait_ge(f_done, c + 3)
                    stored(dve, h_out[u], i, 1)
                    dve.tensor_tensor(hr[:, u, :, :], fr[:, u, :, :], bc_last(dinv[:, bass.ds(c * CB, CB)], D), ALU.mult
                                      ).then_inc(h_done, 1)
            pairs(dve, body)

        @block.gpsimd
        def _(pool):
            def body(i, chunks):
                for u, c, last in chunks:
                    pool.wait_ge(z_done, c + 3)
                    gate(pool, passed)
                    pool.dma_start(rows(z_d, c), zr[:, u, :, :]).then_inc(z_out[u], 16)
                for u, c, last in chunks:
                    pool.wait_ge(h_done, c + 3)
                    gate(pool, passed)
                    pool.dma_start(rows(h_d, c), hr[:, u, :, :]).then_inc(h_out[u], 16)
                    pool.dma_start(rows(feat_d, c), fr[:, u, :, :]).then_inc(f_out[u], 16)
            pairs(pool, body)
            for s in (z_out, f_out, h_out):
                pool.wait_ge(s[0], 16 * (NPAIR + 1))
                pool.wait_ge(s[1], 16 * NPAIR)


def stats(dve, ch, passed, r, st, mv):
    for a in range(CB):
        ins = dve.bn_stats(st[:, a, :], r[:, a, :])
    ch.then(ins)
    gate(dve, passed)
    for a in range(CB):
        ins = dve.bn_aggr(mv[:, a, :], st[:, a, :])
    ch.then(ins)


def normed(dve, ch, r, mv, rstd, z):
    for a in range(CB):
        ins = dve.tensor_scalar(z[:, a, :], r[:, a, :], mv[:, a, 0:1], rstd[:, a:a + 1], ALU.subtract, ALU.mult)
    ch.then(ins)


def dense3(nc, passed, z_d, feat_d, out, GW2, GB2, ident, eps, acc, dinv, psum):
    with ExitStack() as ctx:
        def sb(name, shape, dt=F32):
            return ctx.enter_context(nc.sbuf_tensor(f"d3_{name}", shape, dt))

        def sem(name):
            return ctx.enter_context(nc.semaphore(f"d3_{name}"))

        fr, zr = sb("fr", [P, 2, CB, D]), sb("zr", [P, 2, CB, D])
        aT = sb("aT", [P, 2, CH])
        ag, ur, uT = sb("ag", [P, 2, CB, D]), sb("ur", [P, 2, CB, D]), sb("uT", [P, 2, CH])
        rr, r2, o = sb("rr", [P, 2, CB, D]), sb("r2", [P, 2, CB, D]), sb("o", [P, 2, CB, D])
        st, mv, sd = sb("st", [P, 2, CB, 6]), sb("mv", [P, 2, CB, 2]), sb("sd", [P, 2, 2, CB])
        in_ = [sem(f"in{u}") for u in range(2)]
        o_out = [sem(f"o_out{u}") for u in range(2)]
        aT_done, a_turned, u_done, u_turned, uT_done, v_mm, v_done, var_done, sd_done, o_done, steps = (
            sem(n) for n in ("aT_done", "a_turned", "u_done", "u_turned", "uT_done", "v_mm", "v_done", "var_done", "sd_done",
                             "o_done", "steps"))
        block = ctx.enter_context(nc.Block())
        PA, PU, PV = psum[0:2], psum[2:4], psum[4:6]

        @block.sync
        def _(sync):
            def body(i, chunks):
                for u, c, last in chunks:
                    sync.wait_ge(v_done, c + 1)
                    load_rows(sync, fr[:, u], feat_d, c, last, True, in_[u])
                    load_rows(sync, zr[:, u], z_d, c, last, True, in_[u])
            pairs(sync, body)

        @block.tensor
        def _(pe):
            for s in (a_turned, u_turned, v_mm):
                pe.sem_inc(s, 2)

            def body(i, chunks):
                for u, c, last in chunks:
                    pe.wait_ge(aT_done, c + 1)
                    pe.wait_ge(u_done, c + 1)
                    for a in range(CB):
                        mm = pe.transpose(PA[u][:, a * P:(a + 1) * P], aT[:, u, a * P:(a + 1) * P], ident[:, :])
                    mm.then_inc(a_turned, 1)
                for u, c, last in chunks:
                    pe.wait_ge(u_done, c + 3)
                    pe.wait_ge(uT_done, c + 1)
                    for a in range(CB):
                        mm = pe.transpose(PU[u][:, a * P:(a + 1) * P], ur[:, u, a, :], ident[:, :])
                    mm.then_inc(u_turned, 1)
                for u, c, last in chunks:
                    pe.wait_ge(uT_done, c + 3)
                    pe.wait_ge(v_done, c + 1)
                    for a in range(CB):
                        mm = pe.matmul(PV[u][:, a * D:(a + 1) * D], uT[:, u, a * P:(a + 1) * P], GW2[:, :],
                                       start=True, stop=True)
                    mm.then_inc(v_mm, 1)
            pairs(pe, body)

        @block.scalar
        def _(act):
            act.sem_inc(uT_done, 2)

            def body(i, chunks):
                for u, c, last in chunks:
                    act.wait_ge(a_turned, c + 1)
                    act.copy(aT[:, u, :], acc[:, bass.ds(c * CH, CH)]).then_inc(aT_done, 1)
                for u, c, last in chunks:
                    act.wait_ge(u_turned, c + 3)
                    act.wait_ge(v_mm, c + 1)
                    act.copy(uT[:, u, :], PU[u][:, :]).then_inc(uT_done, 1)
                for u, c, last in chunks:
                    act.wait_ge(var_done, c + 1)
                    act.activation(sd[:, u, 0, :], mv[:, u, :, 1], ACT.Sqrt, bias=eps[:, 0:1]).then_inc(sd_done, 1)
            pairs(act, body)

        @block.vector
        def _(dve):
            for s in (u_done, v_done):
                dve.sem_inc(s, 2)
            b2b = GB2[:, :].unsqueeze(1).broadcast_to([P, CB, D])

            def body(i, chunks):
                ch = Chain(dve, steps, i * (2 * 6))
                for u, c, last in chunks:
                    dve.wait_ge(a_turned, c + 3)
                    dve.wait_ge(in_[u], 64 * i + 64)
                    ch.then(dve.tensor_tensor(ag[:, u, :, :], PA[u][:, :].rearrange("p (a f) -> p a f", a=CB),
                                              bc_last(dinv[:, bass.ds(c * CB, CB)], D), ALU.mult))
                    dve.wait_ge(u_turned, c + 1)
                    dve.tensor_tensor(ur[:, u, :, :], fr[:, u, :, :], ag[:, u, :, :], ALU.subtract).then_inc(u_done, 1)
                for u, c, last in chunks:
                    dve.wait_ge(v_mm, c + 3)
                    dve.tensor_tensor(rr[:, u, :, :], PV[u][:, :].rearrange("p (a f) -> p a f", a=CB), zr[:, u, :, :],
                                      ALU.add).then_inc(v_done, 1)
                    dve.wait_ge(v_done, c + 3)
                    ch.then(dve.tensor_tensor(r2[:, u, :, :], rr[:, u, :, :], b2b, ALU.add))
                    stats(dve, ch, passed, r2[:, u], st[:, u], mv[:, u])
                    dve.sem_inc(var_done, 1)
                for u, c, last in chunks:
                    dve.wait_ge(sd_done, c + 1)
                    ch.then(dve.reciprocal(sd[:, u, 1, :], sd[:, u, 0, :]))
                    stored(dve, o_out[u], i, 2)
                    normed(dve, ch, r2[:, u], mv[:, u], sd[:, u, 1], o[:, u])
                    dve.sem_inc(o_done, 1)
            pairs(dve, body)

        @block.gpsimd
        def _(pool):
            def body(i, chunks):
                for u, c, last in chunks:
                    pool.wait_ge(o_done, c + 1)
                    gate(pool, passed)
                    if last:
                        whole = N - LASTN + P
                        pool.dma_start(out[N - LASTN:whole, :], o[:, u, 0, :]).then_inc(o_out[u], 16)
                        pool.dma_start(out[whole:N, :], o[0:N - whole, u, 1, :]).then_inc(o_out[u], 16)
                    else:
                        for a in range(2):
                            pool.dma_start(rows(out, c)[:, 2 * a:2 * a + 2, :], o[:, u, 2 * a:2 * a + 2, :]
                                           ).then_inc(o_out[u], 16)
            pairs(pool, body)
            pool.wait_ge(o_out[0], 32 * (NPAIR + 1))
            pool.wait_ge(o_out[1], 32 * NPAIR)


_INS = ['x', 'src', 'dst', 'edge_type_8', 'L0_gnn_w1', 'L0_gnn_sl1', 'L0_gnn_b1', 'L0_gnn_w2', 'L0_gnn_sl2',
        'L0_gnn_b2', 'L1_gnn_W1', 'L1_gnn_b1', 'L1_gnn_W2', 'L1_gnn_b2']


def kernel(**inputs):
    import numpy as _np
    import concourse.bacc as _bacc
    from concourse import mybir as _mybir
    from concourse.bass_utils import run_bass_kernel_spmd as _run

    nc = _bacc.Bacc("TRN2", target_bir_lowering=False, num_devices=1)
    arrays, args = {}, []
    for name in _INS:
        a = _np.ascontiguousarray(inputs[name])
        arrays[f"in_{name}_dram"] = a
        args.append(nc.dram_tensor(f"in_{name}_dram", a.shape, _mybir.dt.from_np(a.dtype), kind="ExternalInput").ap())
    o = nc.dram_tensor("out_0_dram", (N, D), _mybir.dt.float32, kind="ExternalOutput").ap()
    build(nc, *args, o)
    r = _run(nc, [arrays], core_ids=[0])
    return r.results[0]["out_0_dram"]
```

```python
import concourse.bass as bass
from concourse import mybir
from contextlib import ExitStack

F32 = mybir.dt.float32
I32 = mybir.dt.int32
BF16 = mybir.dt.bfloat16
ALU = mybir.AluOpType
ACT = mybir.ActivationFunctionType
AX = mybir.AxisListType

P = 128
D = 128
N = 12500
E = 212500
NREL = 8
EPS = 1e-5

KG = 7
GN = 64
TN = 16
TK = TN * NREL
RING = 4
BUFS = 2
UN = RING * KG
TB = 120
NTB = 14
NT = TB * NTB
NG = NT // KG
IT = NG // RING
TILES = -(-E // P)
NO_EDGE = [min(KG, max(0, (NG - RING + h + 1) * KG - TILES)) for h in range(RING)]
assert NT >= TILES > (IT - 1) * UN and IT * RING == NG and NT % KG == 0 and RING % BUFS == 0

CH = 512
CB = CH // P
NCH = -(-N // CH)
NPAD = NCH * CH
NB = NPAD // P
LASTN = N - (NCH - 1) * CH
ACC = NPAD + GN


class Chain:

    def __init__(self, eng, sem, base):
        self.eng, self.sem, self.base, self.n = eng, sem, base, 0

    def then(self, ins):
        ins.then_inc(self.sem, 1)
        self.n += 1
        self.eng.wait_ge(self.sem, self.base + self.n)


def gate(eng, passed):
    eng.sem_inc(passed, 1)


def bc_last(ap, n):
    return ap.unsqueeze(len(ap.shape)).broadcast_to([*ap.shape, n])


def build(nc, x, src, dst, rel, w1, sl1, b1, w2, sl2, b2, gw1, gb1, gw2, gb2, out):
    with ExitStack() as top:
        def sb(name, shape, dt=F32):
            return top.enter_context(nc.sbuf_tensor(name, shape, dt))

        def scratch(name, *shape):
            return nc.dram_tensor(name, shape, F32, kind="Internal").ap()

        tile_lo_d, tile_hi_d = scratch("tile_lo_d", NT), scratch("tile_hi_d", NT)
        x1_d, z_d, feat_d, h_d = (scratch(n, NPAD, D) for n in ("x1_d", "z_d", "feat_d", "h_d"))

        c = Shared()
        c.W = [sb("w1s", [P, NREL, D]), sb("w2s", [P, NREL, D])]
        c.SL = [sb("sl1s", [P, D]), sb("sl2s", [P, D])]
        c.B = [sb("b1s", [P, 1]), sb("b2s", [P, 1])]
        c.GW = [sb("gw1s", [P, D]), sb("gw2s", [P, D])]
        c.GB = [sb("gb1s", [P, D]), sb("gb2s", [P, D])]
        c.ident = sb("ident", [P, P])
        c.iota = sb("iota", [P, TK])
        c.zeros_bf = sb("zeros_bf", [P, CH], BF16)
        c.ones_bf = sb("ones_bf", [P, 1], BF16)
        c.one = sb("one", [1, 1])
        c.eps = sb("eps", [P, 1])
        c.src_i = sb("src_i", [P, NT + UN], I32)
        c.node = sb("node", [P, NT])
        c.relf = sb("relf", [P, NT])
        c.lo_b = sb("lo_b", [P, NT])
        c.glo = sb("glo", [P, NG])
        c.key = sb("key", [P, NT + UN])
        c.gs = sb("gs", [P, NG])
        c.off_i = sb("off_i", [1, NG, KG], I32)
        c.gs_i = sb("gs_i", [1, NG], I32)
        c.step_t, c.step_g, c.carry = sb("step_t", [P, 1]), sb("step_g", [P, 1]), sb("carry", [P, 1])
        c.t = [sb("t1", [P, NT]), sb("t2", [P, NT]), sb("t3", [P, NT], BF16)]
        c.deg = sb("deg", [P, NB])
        c.dinv = sb("dinv", [P, NB])
        c.acc = sb("acc", [P, ACC])
        c.rounds_i = sb("rounds_i", [1, 2], I32)
        c.ends_i = sb("ends_i", [1, 1 + NCH], I32)
        c.passed = top.enter_context(nc.semaphore("passed"))
        c.psum = [top.enter_context(nc.psum_tensor(f"bank{i}", [P, CH], F32)) for i in range(8)]

        prologue(nc, c, x, src, dst, rel, w1, sl1, b1, w2, sl2, b2, gw1, gb1, gw2, gb2, tile_lo_d, tile_hi_d)
        with ExitStack() as ctx:
            cnt = ctx.enter_context(nc.sbuf_tensor("cnt", [1, ACC], F32))
            tail = Tail1(nc, ctx, c, x, x1_d, cnt)
            relational_sum(nc, ctx, c, "r1", x, c.W[0], cnt, tail)
        with ExitStack() as ctx:
            tail = Tail2(nc, ctx, c, x, x1_d, z_d, feat_d, h_d)
            relational_sum(nc, ctx, c, "r2", x1_d, c.W[1], None, tail)
        with ExitStack() as ctx:
            tail = Tail3(nc, ctx, c, z_d, feat_d, out)
            plain_sum(nc, ctx, c, h_d, tail)


class Shared:
    pass


def prologue(nc, c, x, src, dst, rel, w1, sl1, b1, w2, sl2, b2, gw1, gb1, gw2, gb2, tile_lo_d, tile_hi_d):
    with ExitStack() as ctx:
        def sb(name, shape, dt=F32):
            return ctx.enter_context(nc.sbuf_tensor(name, shape, dt))

        def sem(name):
            return ctx.enter_context(nc.semaphore(name))

        raw = [sb(f"raw{n}", [TB, NTB, P], I32) for n in ("d", "r", "s")]
        rawf = [sb(f"rawf{n}", [TB, NTB, P]) for n in ("d", "r", "s")]
        tlo, thi = sb("tlo", [TB, NTB]), sb("thi", [TB, NTB])
        hi_b = sb("hi_b", [P, NT])
        span = sb("span", [P, NT])
        ghi = sb("ghi", [P, NG])
        sp = sb("sp", [P, 8])
        spi = sb("spi", [P, 8], I32)
        ilo, done, ends = sb("ilo", [P, IT]), sb("done", [P, IT]), sb("ends", [P, 1])
        count, above = sb("count", [P, IT]), sb("above", [P, 1])
        ends_ready, ends_turned = sem("ends_ready"), sem("ends_turned")
        padded, raw_in, consts, ident0 = sem("padded"), sem("raw_in"), sem("consts"), sem("ident0")
        weights_in, conv, turned, placed = sem("weights_in"), sem("conv"), sem("turned"), sem("placed")
        tile_out, tile_in, steps = sem("tile_out"), sem("tile_in"), sem("steps")
        block = ctx.enter_context(nc.Block())

        full = E // P
        before = (NTB - 1) * TB
        pads = (N, 0, 0)

        @block.sync
        def _(sync):
            sync.wait_ge(padded, 3)
            for a, r in zip((dst, rel, src), raw):
                sync.dma_start(r[:, 0:NTB - 1, :], a[0:before * P].rearrange("(j p e) -> p j e", j=NTB - 1, p=TB)
                               ).then_inc(raw_in, 16)
                sync.dma_start(r[0:full - before, NTB - 1, :],
                               a[before * P:full * P].rearrange("(p e) -> p e", e=P)).then_inc(raw_in, 16)
                sync.dma_start(r[full - before:full - before + 1, NTB - 1, 0:E - full * P],
                               a[full * P:E].rearrange("(p e) -> p e", p=1)).then_inc(raw_in, 16)
            loads = [(c.W[0], w1.rearrange("r i o -> i r o")), (c.W[1], w2.rearrange("r i o -> i r o")),
                     (c.SL[0], sl1), (c.SL[1], sl2), (c.GW[0], gw1), (c.GW[1], gw2),
                     (c.B[0], b1.rearrange("(p a) -> p a", a=1)), (c.B[1], b2.rearrange("(p a) -> p a", a=1)),
                     (c.GB[0], gb1.partition_broadcast(P)), (c.GB[1], gb2.partition_broadcast(P))]
            for to, of in loads:
                sync.dma_start(to[:], of).then_inc(weights_in, 16)
            sync.wait_ge(weights_in, 16 * len(loads))
            sync.wait_ge(conv, 5)
            sync.dma_start(tile_lo_d.rearrange("(j p) -> p j", p=TB), tlo[:, :],
                           allow_slow_non_contiguous=True).then_inc(tile_out, 16)
            sync.dma_start(tile_hi_d.rearrange("(j p) -> p j", p=TB), thi[:, :],
                           allow_slow_non_contiguous=True).then_inc(tile_out, 16)
            sync.wait_ge(tile_out, 32)
            sync.dma_start(c.lo_b[:, :], tile_lo_d.partition_broadcast(P)).then_inc(tile_in, 16)
            sync.dma_start(hi_b[:, :], tile_hi_d.partition_broadcast(P)).then_inc(tile_in, 16)

        @block.gpsimd
        def _(pool):
            nc.gpsimd.memset(c.ident[:, :], 0.0).then_inc(ident0, 1)
            pool.wait_ge(ident0, 1)
            nc.gpsimd.affine_select(out=c.ident[:, :], in_=c.ident[:, :], compare_op=ALU.not_equal, fill=1.0, base=0,
                                    pattern=[[-1, P]], channel_multiplier=1).then_inc(consts, 1)
            nc.gpsimd.iota(count[:, :], [[1, IT]], base=1, channel_multiplier=0,
                           allow_small_or_imprecise_dtypes=True).then_inc(consts, 1)
            nc.gpsimd.iota(above[:, :], [[1, 1]], base=CH, channel_multiplier=CH,
                           allow_small_or_imprecise_dtypes=True).then_inc(consts, 1)
            nc.gpsimd.iota(c.iota[:, :], [[1, TK]], base=0, channel_multiplier=0,
                           allow_small_or_imprecise_dtypes=True).then_inc(consts, 1)

        @block.vector
        def _(dve):
            for r, pad in zip(raw, pads):
                dve.memset(r[:, NTB - 1, :], pad).then_inc(padded, 1)
            dve.memset(c.zeros_bf[:, :], 0.0).then_inc(consts, 1)
            dve.memset(c.ones_bf[:, :], 1.0).then_inc(consts, 1)
            dve.memset(c.one[:, :], 1.0).then_inc(consts, 1)
            dve.memset(c.eps[:, :], EPS).then_inc(consts, 1)
            dve.memset(c.src_i[:, NT:], 0).then_inc(consts, 1)
            dve.memset(c.key[:, NT:], -1.0).then_inc(consts, 1)
            dve.memset(c.ends_i[:, 0:1], 0).then_inc(consts, 1)
            dve.memset(c.step_t[:, :], 0.0).then_inc(consts, 1)
            dve.memset(c.step_g[:, :], 0.0).then_inc(consts, 1)
            dve.wait_ge(raw_in, 16 * 9)
            for r, f in zip(raw, rawf):
                dve.tensor_copy(f[:, :, :], r[:, :, :]).then_inc(conv, 1)
            dve.wait_ge(conv, 3)
            dve.tensor_reduce(tlo[:, :], rawf[0][:, :, :], AX.X, ALU.min).then_inc(conv, 1)
            dve.tensor_reduce(thi[:, :], rawf[0][:, :, :], AX.X, ALU.max).then_inc(conv, 1)
            for b, (to, j0) in enumerate(banks_of((c.node, c.relf, c.src_i))):
                n = min(4, NTB - j0) * TB
                dve.wait_ge(turned, b + 1)
                dve.tensor_copy(to[:, j0 * TB:j0 * TB + n], c.psum[b % 8][:, 0:n]).then_inc(placed, 1)
            dve.wait_ge(tile_in, 32)
            ch = Chain(dve, steps, 0)
            ch.then(dve.tensor_reduce(c.glo[:, :], c.lo_b[:, :].rearrange("p (g k) -> p g k", k=KG), AX.X, ALU.min))
            ch.then(dve.tensor_reduce(ghi[:, :], hi_b[:, :].rearrange("p (g k) -> p g k", k=KG), AX.X, ALU.max))
            ch.then(dve.tensor_tensor(span[:, :], hi_b[:, :], c.lo_b[:, :], ALU.subtract))
            ch.then(dve.tensor_reduce(sp[:, 0:1], span[:, :], AX.X, ALU.max))
            ch.then(dve.tensor_tensor(ghi[:, :], ghi[:, :], c.glo[:, :], ALU.subtract))
            ch.then(dve.tensor_reduce(sp[:, 1:2], ghi[:, :], AX.X, ALU.max))
            ch.then(dve.tensor_copy(spi[:, 0:1], sp[:, 1:2]))
            ch.then(dve.tensor_scalar(spi[:, 1:2], spi[:, 0:1], 6, None, ALU.arith_shift_right))
            ch.then(dve.tensor_copy(sp[:, 2:3], spi[:, 1:2]))
            ch.then(dve.tensor_scalar(sp[:, 3:4], sp[:, 2:3], 1.0, None, ALU.add))
            ch.then(dve.tensor_scalar(sp[:, 4:5], sp[:, 0:1], float(TN), None, ALU.is_ge))
            ch.then(dve.tensor_scalar(sp[:, 5:6], sp[:, 1:2], float(GN), None, ALU.is_ge))
            ch.then(dve.tensor_tensor(sp[:, 4:5], sp[:, 4:5], sp[:, 5:6], ALU.max))
            ch.then(dve.tensor_scalar(sp[:, 5:6], sp[:, 3:4], float(GN // TN), -1.0, ALU.mult, ALU.add))
            ch.then(dve.tensor_tensor(sp[:, 5:6], sp[:, 5:6], sp[:, 4:5], ALU.mult))
            ch.then(dve.tensor_scalar(sp[:, 2:3], sp[:, 5:6], 1.0, None, ALU.add))
            ch.then(dve.tensor_copy(c.rounds_i[:, :], sp[0:1, 2:4]))
            ch.then(dve.tensor_reduce(ilo[:, :], c.glo[:, :].rearrange("p (i h) -> p i h", h=RING), AX.X, ALU.min))
            dve.wait_ge(consts, 13)
            ch.then(dve.scalar_tensor_tensor(done[:, :], ilo[:, :], above[:, 0:1], count[:, :], ALU.is_lt, ALU.mult))
            dve.tensor_reduce(ends[:, :], done[:, :], AX.X, ALU.max).then_inc(ends_ready, 1)
            windows(dve, c, ch)
            dve.wait_ge(ends_turned, 1)
            dve.tensor_copy(c.ends_i[0:1, 1:1 + NCH], c.psum[7][0:1, 0:NCH]).then_inc(ends_ready, 1)

        @block.tensor
        def _(pe):
            pe.wait_ge(conv, 3)
            pe.wait_ge(consts, 13)
            b = 0
            for n, (to, j0) in enumerate(banks_of((0, 1, 2))):
                if n >= 8:
                    pe.wait_ge(placed, n - 7)
                for j in range(j0, min(j0 + 4, NTB)):
                    mm = pe.transpose(c.psum[n % 8][:, (j - j0) * TB:(j - j0 + 1) * TB], rawf[to][:, j, :],
                                      c.ident[0:TB, 0:TB])
                mm.then_inc(turned, 1)
            pe.wait_ge(placed, len(banks_of((0, 1, 2))))
            pe.wait_ge(ends_ready, 1)
            pe.transpose(c.psum[7][0:1, 0:P], ends[:, 0:1], c.ident[:, :]).then_inc(ends_turned, 1)


def banks_of(tensors):
    return [(t, j0) for t in tensors for j0 in range(0, NTB, 4)]


def windows(dve, c, ch):
    t1, t2, t3 = c.t
    by_group = lambda a: a[:, 0:NT].rearrange("p (g k) -> p g k", k=KG)
    gsb = bc_last(c.gs[:, :], KG)
    n = ch.n
    ch.then(dve.tensor_scalar(c.gs[:, :], c.glo[:, :], c.step_g[:, 0:1], None, ALU.add))
    ch.then(dve.tensor_tensor(by_group(t1), by_group(c.lo_b), gsb, ALU.max))
    ch.then(dve.tensor_scalar(t1[:, :], t1[:, :], c.step_t[:, 0:1], None, ALU.add))
    ch.then(dve.scalar_tensor_tensor(by_group(t2), gsb, float(GN - TN), by_group(t1), ALU.add, ALU.min))
    ch.then(dve.tensor_tensor(by_group(t3)[0:1, :, :], by_group(t2)[0:1, :, :], gsb[0:1, :, :], ALU.subtract))
    ch.then(dve.tensor_scalar(c.off_i[0:1, :, 0:KG], by_group(t3)[0:1, :, :], float(NREL), None, ALU.mult))
    ch.then(dve.tensor_scalar(c.gs_i[:, :], c.gs[0:1, :], float(NPAD), None, ALU.min))
    ch.then(dve.tensor_tensor(t1[:, :], c.node[:, :], t1[:, :], ALU.subtract))
    ch.then(dve.tensor_scalar(t3[:, :], t1[:, :], 0.0, None, ALU.is_ge))
    ch.then(dve.scalar_tensor_tensor(t3[:, :], t1[:, :], float(TN), t3[:, :], ALU.is_lt, ALU.mult))
    ch.then(dve.tensor_tensor(by_group(t1), by_group(c.node), gsb, ALU.subtract))
    ch.then(dve.scalar_tensor_tensor(t3[:, :], t1[:, :], float(GN), t3[:, :], ALU.is_lt, ALU.mult))
    ch.then(dve.tensor_tensor(t1[:, :], c.node[:, :], t2[:, :], ALU.subtract))
    ch.then(dve.scalar_tensor_tensor(t1[:, :], t1[:, :], float(NREL), c.relf[:, :], ALU.mult, ALU.add))
    ch.then(dve.scalar_tensor_tensor(t1[:, :], t1[:, :], 1.0, t3[:, :], ALU.add, ALU.mult))
    ch.then(dve.tensor_scalar(c.key[:, 0:NT], t1[:, :], -1.0, None, ALU.add))
    ch.then(dve.tensor_scalar(c.step_t[:, :], c.step_t[:, :], float(TN), None, ALU.add))
    ch.then(dve.tensor_scalar(c.carry[:, :], c.step_t[:, :], float(GN), float(GN), ALU.is_ge, ALU.mult))
    ch.then(dve.tensor_tensor(c.step_t[:, :], c.step_t[:, :], c.carry[:, :], ALU.subtract))
    ch.then(dve.tensor_tensor(c.step_g[:, :], c.step_g[:, :], c.carry[:, :], ALU.add))
    assert ch.n - n == WINDOW_STEPS


WINDOW_STEPS = 20


def by_chunk(eng, c, iteration, dense):
    def reach(k):
        since = eng.value_load(c.ends_i[0:1, bass.ds(k, 1)], min_val=0, max_val=IT)
        until = eng.value_load(c.ends_i[0:1, bass.ds(k + 1, 1)], min_val=0, max_val=IT)
        with eng.If(since < until):
            with eng.Fori(since, until) as i:
                iteration(i)
        eng.end_ifs()

    with eng.Fori(0, NCH - 1) as k:
        reach(k)
        dense(k, False)
    reach(NCH - 1)
    dense(NCH - 1, True)


def rounds_of(eng, c, which, most):
    return eng.value_load(c.rounds_i[0:1, which:which + 1], min_val=1, max_val=most)


class Gathers:

    def __init__(self, nc, ctx, c, tag, table, which, most):
        def sem(name):
            return ctx.enter_context(nc.semaphore(f"{tag}_{name}"))

        self.nc, self.c, self.table, self.which, self.most = nc, c, table, which, most
        self.rows = ctx.enter_context(nc.sbuf_tensor(f"{tag}_rows", [P, UN, D], F32))
        self.idx = ctx.enter_context(nc.sbuf_tensor(f"{tag}_idx", [P, UN], I32))
        self.landed = [sem(f"landed{h}") for h in range(RING)]
        self.idx_ready = [sem(f"idx_ready{h}") for h in range(RING)]
        self.summed = [sem(f"summed{h}") for h in range(RING)]

    def start(self, pe):
        for h in range(RING):
            pe.sem_inc(self.summed[h], 1)

    def take(self, act, h, q, i):
        act.wait_ge(self.summed[h], q * IT + i + 1)
        act.copy(self.idx[:, h * KG:(h + 1) * KG], self.c.src_i[:, bass.ds(i * UN + h * KG, KG)]
                 ).then_inc(self.idx_ready[h], 1)

    def run(self, pool):
        rounds = rounds_of(pool, self.c, self.which, self.most)

        def iteration(q, i, skipped):
            for h in range(RING):
                pool.wait_ge(self.idx_ready[h], q * (IT + 1) + i + 1)
                pool.wait_ge(self.summed[h], q * IT + i + 1)
                gate(pool, self.c.passed)
                for s in range(h * KG, (h + 1) * KG - skipped[h]):
                    pool.indirect_dma_start(
                        out=self.rows[:, s, :], out_offset=None, in_=self.table[:, :],
                        in_offset=bass.IndirectOffsetOnAxis(ap=self.idx[:, s:s + 1], axis=0)
                    ).then_inc(self.landed[h], 16)

        with pool.Fori(0, rounds) as q:
            with pool.Fori(0, IT - 1) as i:
                iteration(q, i, [0] * RING)
            iteration(q, IT - 1, NO_EDGE)

    def wait_rows(self, pe, h, q, i):
        tiles = q * (IT * KG - NO_EDGE[h]) + i * KG + (KG - NO_EDGE[h])
        if NO_EDGE[h]:
            tiles = tiles + (i < IT - 1) * NO_EDGE[h]
        pe.wait_ge(self.landed[h], tiles * 16)


def behind(sems, h, n):
    b = (h - BUFS) % RING
    return sems[b], n + (2 if b < h else 1)


def relational_sum(nc, ctx, c, tag, table, W, cnt, tail):
    def sb(name, shape, dt=F32):
        return ctx.enter_context(nc.sbuf_tensor(f"{tag}_{name}", shape, dt))

    def sem(name):
        return ctx.enter_context(nc.semaphore(f"{tag}_{name}"))

    most = 4 * (N // GN + 1)
    g = Gathers(nc, ctx, c, tag, table, 0, most)
    summed = g.summed
    S = sb("S", [P, BUFS, KG, TK])
    agg = sb("agg", [P, BUFS, GN, NREL])
    dsum = sb("dsum", [1, GN])
    hot_ready = [sem(f"hot_ready{h}") for h in range(RING)]
    agg_out = [sem(f"agg_out{h}") for h in range(RING)]
    mixed = [sem(f"mixed{h}") for h in range(RING)]
    added = [sem(f"added{h}") for h in range(RING)]
    tables, steps, table_steps, setup = sem("tables"), sem("steps"), sem("table_steps"), sem("setup")
    agg_ps, mix_ps, cnt_ps = c.psum[0:2], c.psum[2:4], c.psum[4:6]
    block = ctx.enter_context(nc.Block())

    @block.sync
    def _(sync):
        tail.sync(sync, rounds_of(sync, c, 0, most))

    @block.scalar
    def _(act):
        rounds = rounds_of(act, c, 0, most)
        tail.start_act(act)
        with act.Fori(0, rounds) as q:
            for h in range(RING):
                g.take(act, h, q, 0)

            def iteration(i):
                n = act.snap(q * IT + i)
                for h in range(RING):
                    b = h % BUFS
                    act.wait_ge(summed[h], n + 2)
                    act.wait_ge(*behind(mixed, h, n))
                    act.copy(agg[:, b, :, :], agg_ps[b][:, :].rearrange("p (n r) -> p n r", r=NREL)
                             ).then_inc(agg_out[h], 1)
                    g.take(act, h, q, i + 1)
            by_chunk(act, c, iteration, lambda k, last: tail.act(act, k, q * NCH + k, last))
        tail.end_act(act)

    @block.gpsimd
    def _(pool):
        g.run(pool)

    @block.tensor
    def _(pe):
        g.start(pe)
        for h in range(RING):
            pe.sem_inc(mixed[h], 1)
        rounds = rounds_of(pe, c, 0, most)
        with pe.Fori(0, rounds) as q:
            pe.wait_ge(tables, q + 1)
            gate(pe, c.passed)

            def iteration(i):
                n = pe.snap(q * IT + i)

                def mix(h):
                    b = h % BUFS
                    pe.wait_ge(agg_out[h], n + 2)
                    pe.wait_ge(*behind(added, h, n))
                    for r in range(NREL):
                        mm = pe.matmul(mix_ps[b][:, 0:GN], W[:, r, :], agg[:, b, :, r],
                                       start=(r == 0), stop=(r == NREL - 1))
                    mm.then_inc(mixed[h], 1)

                for h in range(RING):
                    b = h % BUFS
                    _, offs = nc.values_load_multi_w_load_instructions(
                        c.off_i[0:1, bass.ds(i * RING + h, 1), :], engines=bass.OrderedEngineSet([pe.engine]),
                        min_val=0, max_val=(GN - TN) * NREL, skip_runtime_bounds_check_because="clamped on the chip")
                    pe.wait_ge(*behind(agg_out, h, n))
                    pe.matmul(agg_ps[b][:, :], c.zeros_bf[:, 0:P], c.zeros_bf[:, :], start=True, stop=False,
                              skip_group_check=True)
                    if cnt is not None:
                        pe.wait_ge(*behind(added, h, n))
                        pe.matmul(cnt_ps[b][0:1, :], c.zeros_bf[:, 0:1], c.zeros_bf[:, :], start=True, stop=False,
                                  skip_group_check=True)
                    pe.wait_ge(hot_ready[h], n + 1 + (q if h < BUFS else 0))
                    g.wait_rows(pe, h, q, i)
                    for k in range(KG):
                        mm = pe.matmul(agg_ps[b][:, bass.ds(offs[k], TK)], g.rows[:, h * KG + k, :], S[:, b, k, :],
                                       start=False, stop=(k == KG - 1), skip_group_check=True)
                        if cnt is not None:
                            mm = pe.matmul(cnt_ps[b][0:1, bass.ds(offs[k], TK)], c.ones_bf[:, :],
                                           S[:, b, k, :].bitcast(BF16)[:, 1:2 * TK:2],
                                           start=False, stop=(k == KG - 1), skip_group_check=True)
                    mm.then_inc(summed[h], 1)
                    if h > 0:
                        mix(h - 1)
                mix(RING - 1)
            by_chunk(pe, c, iteration, lambda k, last: tail.pe(pe, k, q * NCH + k, last))

    @block.vector
    def _(dve):
        for h in range(RING):
            dve.sem_inc(added[h], 1)
            dve.sem_inc(agg_out[h], 1)
        tail.start_dve(dve)
        rounds = rounds_of(dve, c, 0, most)
        with dve.If(rounds > 1):
            dve.memset(c.step_t[:, :], 0.0).then_inc(setup, 1)
            dve.memset(c.step_g[:, :], 0.0).then_inc(setup, 1)
            dve.wait_ge(setup, 2)
            gate(dve, c.passed)
        dve.end_ifs()
        dve.memset(c.acc[:, :], 0.0).then_inc(setup, 1)
        if cnt is not None:
            dve.memset(cnt[:, :], 0.0).then_inc(setup, 1)

        def one_hot(h, q, i):
            dve.wait_ge(*behind(summed, h, q * IT + i))
            dve.tensor_tensor(
                S[:, h % BUFS, :, :], c.iota[:, :].unsqueeze(1).broadcast_to([P, KG, TK]),
                bc_last(c.key[:, bass.ds(i * UN + h * KG, KG)], TK), ALU.is_equal).then_inc(hot_ready[h], 1)

        per_iter = RING * (1 if cnt is None else 3)
        with dve.Fori(0, rounds) as q:
            with dve.If(rounds > 1):
                windows(dve, c, Chain(dve, table_steps, q * WINDOW_STEPS))
                gate(dve, c.passed)
            dve.end_ifs()
            dve.sem_inc(tables, 1)
            for h in range(BUFS):
                one_hot(h, q, 0)
            dve.wait_ge(setup, 1 if cnt is None else 2)
            gate(dve, c.passed)

            def iteration(i):
                n = dve.snap(q * IT + i)
                ch = Chain(dve, steps, n * per_iter)
                for h in range(RING):
                    b = h % BUFS
                    g0 = dve.value_load(c.gs_i[0:1, bass.ds(i * RING + h, 1)], min_val=0, max_val=NPAD)
                    if cnt is not None:
                        dve.wait_ge(summed[h], n + 2)
                        ch.then(dve.tensor_reduce(dsum[:, :], cnt_ps[b][0:1, :].rearrange("p (n r) -> p n r", r=NREL),
                                                  AX.X, ALU.add))
                        window = cnt[:, bass.ds(g0, GN)]
                        ch.then(dve.tensor_tensor(window, window, dsum[:, :], ALU.add))
                    one_hot((h + BUFS) % RING, q, i + (h + BUFS) // RING)
                    dve.wait_ge(mixed[h], n + 2)
                    window = c.acc[:, bass.ds(g0, GN)]
                    ch.then(dve.tensor_tensor(window, window, mix_ps[b][:, 0:GN], ALU.add))
                    dve.sem_inc(added[h], 1)
                assert ch.n == per_iter
            by_chunk(dve, c, iteration, lambda k, last: tail.dve(dve, k, q * NCH + k, last))
        tail.end_dve(dve)


def plain_sum(nc, ctx, c, table, tail):
    tag = "r3"

    def sb(name, shape, dt=F32):
        return ctx.enter_context(nc.sbuf_tensor(f"{tag}_{name}", shape, dt))

    def sem(name):
        return ctx.enter_context(nc.semaphore(f"{tag}_{name}"))

    most = N // GN + 1
    g = Gathers(nc, ctx, c, tag, table, 1, most)
    summed = g.summed
    S = sb("S", [P, BUFS, KG, GN])
    hot_ready = [sem(f"hot_ready{h}") for h in range(RING)]
    added = [sem(f"added{h}") for h in range(RING)]
    steps, table_steps, setup = sem("steps"), sem("table_steps"), sem("setup")
    sum_ps = c.psum[0:2]
    block = ctx.enter_context(nc.Block())

    @block.sync
    def _(sync):
        tail.sync(sync, rounds_of(sync, c, 1, most))

    @block.scalar
    def _(act):
        rounds = rounds_of(act, c, 1, most)
        tail.start_act(act)
        with act.Fori(0, rounds) as q:
            for h in range(RING):
                g.take(act, h, q, 0)

            def iteration(i):
                for h in range(RING):
                    g.take(act, h, q, i + 1)
            by_chunk(act, c, iteration, lambda k, last: tail.act(act, k, q * NCH + k, last))
        tail.end_act(act)

    @block.gpsimd
    def _(pool):
        g.run(pool)

    @block.tensor
    def _(pe):
        g.start(pe)
        rounds = rounds_of(pe, c, 1, most)
        with pe.Fori(0, rounds) as q:
            def iteration(i):
                n = pe.snap(q * IT + i)
                for h in range(RING):
                    b = h % BUFS
                    pe.wait_ge(*behind(added, h, n))
                    pe.wait_ge(hot_ready[h], n + 1 + (q if h < BUFS else 0))
                    g.wait_rows(pe, h, q, i)
                    for k in range(KG):
                        mm = pe.matmul(sum_ps[b][:, 0:GN], g.rows[:, h * KG + k, :], S[:, b, k, :], start=(k == 0),
                                       stop=(k == KG - 1))
                    mm.then_inc(summed[h], 1)
            by_chunk(pe, c, iteration, lambda k, last: tail.pe(pe, k, q * NCH + k, last))

    @block.vector
    def _(dve):
        for h in range(RING):
            dve.sem_inc(added[h], 1)
        tail.start_dve(dve)
        dve.memset(c.step_g[:, :], 0.0).then_inc(setup, 1)
        dve.wait_ge(setup, 1)
        rounds = rounds_of(dve, c, 1, most)
        dve.memset(c.acc[:, :], 0.0).then_inc(setup, 1)

        def one_hot(h, q, i):
            dve.wait_ge(*behind(summed, h, q * IT + i))
            dve.tensor_tensor(
                S[:, h % BUFS, :, :], c.iota[:, 0:GN].unsqueeze(1).broadcast_to([P, KG, GN]),
                bc_last(c.key[:, bass.ds(i * UN + h * KG, KG)], GN), ALU.is_equal).then_inc(hot_ready[h], 1)

        per_table = 4
        with dve.Fori(0, rounds) as q:
            ch = Chain(dve, table_steps, q * per_table)
            ch.then(dve.tensor_scalar(c.gs[:, :], c.glo[:, :], c.step_g[:, 0:1], None, ALU.add))
            ch.then(dve.tensor_scalar(c.gs_i[:, :], c.gs[0:1, :], float(NPAD), None, ALU.min))
            ch.then(dve.tensor_tensor(c.key[:, 0:NT].rearrange("p (g k) -> p g k", k=KG),
                                      c.node[:, :].rearrange("p (g k) -> p g k", k=KG), bc_last(c.gs[:, :], KG),
                                      ALU.subtract))
            ch.then(dve.tensor_scalar(c.step_g[:, :], c.step_g[:, :], float(GN), None, ALU.add))
            assert ch.n == per_table
            for h in range(BUFS):
                one_hot(h, q, 0)
            dve.wait_ge(setup, 2)
            gate(dve, c.passed)

            def iteration(i):
                n = dve.snap(q * IT + i)
                ch = Chain(dve, steps, n * RING)
                for h in range(RING):
                    g0 = dve.value_load(c.gs_i[0:1, bass.ds(i * RING + h, 1)], min_val=0, max_val=NPAD)
                    dve.wait_ge(summed[h], n + 2)
                    window = c.acc[:, bass.ds(g0, GN)]
                    ch.then(dve.tensor_tensor(window, window, sum_ps[h % BUFS][:, 0:GN], ALU.add))
                    dve.sem_inc(added[h], 1)
                    one_hot((h + BUFS) % RING, q, i + (h + BUFS) // RING)
            by_chunk(dve, c, iteration, lambda k, last: tail.dve(dve, k, q * NCH + k, last))
        tail.end_dve(dve)


def rows(table, k):
    return table[bass.ds(k * CH, CH), :].rearrange("(a p) f -> p a f", p=P)


def load_rows(eng, to, table, k, last, padded_table, landed):
    if last and not padded_table:
        part = LASTN % P
        assert LASTN // P == 1
        eng.dma_start(to[:, 0, :], table[N - LASTN:N - part, :]).then_inc(landed, 16)
        eng.dma_start(to[0:part, 1, :], table[N - part:N, :]).then_inc(landed, 16)
    else:
        for a in range(2):
            eng.dma_start(to[:, 2 * a:2 * a + 2, :], rows(table, k)[:, 2 * a:2 * a + 2, :]).then_inc(landed, 16)


def prefetched(sync, rounds, load, store):
    with sync.Fori(0, rounds) as q:
        m = sync.snap(q * NCH)
        load(0, m, False)
        with sync.Fori(1, NCH - 1) as k:
            m = sync.snap(q * NCH + k)
            load(k, m, False)
            store(k - 1, m - 1, False)
        m = sync.snap(q * NCH + (NCH - 1))
        load(NCH - 1, m, True)
        store(NCH - 2, m - 1, False)
        store(NCH - 1, m, True)


def blocks(ap):
    return ap.rearrange("p (a f) -> p a f", a=CB)


class Tail1:

    def __init__(self, nc, ctx, c, x, x1_d, cnt):
        def sb(name, shape):
            return ctx.enter_context(nc.sbuf_tensor(f"d1_{name}", shape, F32))

        def sem(name):
            return ctx.enter_context(nc.semaphore(f"d1_{name}"))

        self.c, self.x, self.x1_d, self.cnt = c, x, x1_d, cnt
        self.xr, self.yr = sb("xr", [P, CB, D]), sb("yr", [P, CB, D])
        self.xT = self.pre = self.yT = sb("xT", [P, CH])
        self.cntc = sb("cntc", [1, CH])
        (self.x_in, self.x_turned, self.xT_done, self.selfed, self.pre_done, self.y_act, self.y_turned, self.y_done,
         self.y_out, self.y_stored, self.whole, self.cnt_done, self.counts, self.degs) = (
            sem(n) for n in ("x_in", "x_turned", "xT_done", "selfed", "pre_done", "y_act", "y_turned", "y_done",
                             "y_out", "y_stored", "whole", "cnt_done", "counts", "degs"))
        self.PT = self.PO = c.psum[6]
        self.PS = c.psum[7]
        self.PD = c.psum[2][:, GN:GN + CB]

    def sync(self, sync, rounds):
        sync.sem_inc(self.x_turned, 1)
        sync.sem_inc(self.y_stored, 1)

        def load(k, m, last):
            sync.wait_ge(self.x_turned, m + 1)
            load_rows(sync, self.xr, self.x, k, last, False, self.x_in)

        def store(k, m, last):
            sync.wait_ge(self.y_done, m + 2)
            sync.dma_start(rows(self.x1_d, k), self.yr[:, :, :]).then_inc(self.y_out, 16)
            sync.wait_ge(self.y_out, m * 16 + 16)
            sync.sem_inc(self.y_stored, 1)
        prefetched(sync, rounds, load, store)

    def pe(self, pe, k, m, last):
        pe.wait_ge(self.x_in, m * 32 + 32)
        pe.wait_ge(self.y_done, m + 1)
        for a in range(CB):
            mm = pe.transpose(self.PT[:, a * P:(a + 1) * P], self.xr[:, a, :], self.c.ident[:, :])
        mm.then_inc(self.x_turned, 1)
        pe.wait_ge(self.cnt_done, m + 1)
        for a in range(CB):
            mm = pe.matmul(self.PD[:, a:a + 1], self.cntc[0:1, a * P:(a + 1) * P], self.c.one[:, :],
                           start=True, stop=True)
        mm.then_inc(self.counts, 1)
        pe.wait_ge(self.xT_done, m + 1)
        pe.matmul(self.PS[:, :], self.c.SL[0][:, :], self.xT[:, :], start=True, stop=True).then_inc(self.selfed, 1)
        pe.wait_ge(self.y_act, m + 1)
        for a in range(CB):
            mm = pe.transpose(self.PO[:, a * P:(a + 1) * P], self.yT[:, a * P:(a + 1) * P], self.c.ident[:, :])
        mm.then_inc(self.y_turned, 1)

    def start_act(self, act):
        pass

    def act(self, act, k, m, last):
        act.wait_ge(self.whole, m + 1)
        act.copy(self.cntc[:, :], self.cnt[:, bass.ds(k * CH, CH)]).then_inc(self.cnt_done, 1)
        act.wait_ge(self.x_turned, m + 2)
        act.copy(self.xT[:, :], self.PT[:, :]).then_inc(self.xT_done, 1)
        act.wait_ge(self.pre_done, m + 1)
        act.activation(self.yT[:, :], self.pre[:, :], ACT.Relu, bias=self.c.B[0][:, 0:1]).then_inc(self.y_act, 1)

    def end_act(self, act):
        act.wait_ge(self.degs, 1)
        act.activation(self.c.deg[:, :], self.c.deg[:, :], ACT.Sqrt).then_inc(self.degs, 1)

    def start_dve(self, dve):
        dve.sem_inc(self.y_done, 1)

    def dve(self, dve, k, m, last):
        dve.sem_inc(self.whole, 1)
        dve.wait_ge(self.counts, m + 1)
        dve.tensor_scalar(self.c.deg[:, bass.ds(k * CB, CB)], self.PD, 1.0, None, ALU.max)
        dve.wait_ge(self.selfed, m + 1)
        dve.tensor_tensor(self.pre[:, :], self.PS[:, :], self.c.acc[:, bass.ds(k * CH, CH)], ALU.add
                          ).then_inc(self.pre_done, 1)
        dve.wait_ge(self.y_turned, m + 1)
        dve.wait_ge(self.y_stored, m + 1)
        dve.tensor_copy(self.yr[:, :, :], blocks(self.PO[:, :])).then_inc(self.y_done, 1)

    def end_dve(self, dve):
        dve.sem_inc(self.degs, 1)
        dve.wait_ge(self.degs, 2)
        dve.reciprocal(self.c.dinv[:, :], self.c.deg[:, :]).then_inc(self.degs, 1)


class Tail2:

    def __init__(self, nc, ctx, c, x, x1_d, z_d, feat_d, h_d):
        def sb(name, shape):
            return ctx.enter_context(nc.sbuf_tensor(f"d2_{name}", shape, F32))

        def sem(name):
            return ctx.enter_context(nc.semaphore(f"d2_{name}"))

        self.c, self.x, self.x1_d, self.z_d, self.feat_d, self.h_d = c, x, x1_d, z_d, feat_d, h_d
        self.x1r, self.xr, self.rr, self.zr, self.fp, self.fr, self.hr = (
            sb(n, [P, CB, D]) for n in ("x1r", "xr", "rr", "zr", "fp", "fr", "hr"))
        self.xT, self.pre, self.yT, self.zT = (sb(n, [P, CH]) for n in ("xT", "pre", "yT", "zT"))
        self.st, self.mv, self.sd = sb("st", [P, CB, 6]), sb("mv", [P, CB, 2]), sb("sd", [P, 2, CB])
        (self.x_in, self.x_turned, self.xT_done, self.selfed, self.pre_done, self.y_act, self.y_turned, self.res_done,
         self.var_done, self.sd_done, self.z_done, self.z_turned, self.zT_done, self.f_mm, self.f_pre, self.f_done,
         self.h_done, self.out, self.stored, self.steps) = (
            sem(n) for n in ("x_in", "x_turned", "xT_done", "selfed", "pre_done", "y_act", "y_turned", "res_done",
                             "var_done", "sd_done", "z_done", "z_turned", "zT_done", "f_mm", "f_pre", "f_done",
                             "h_done", "out", "stored", "steps"))
        self.PT = self.PF = c.psum[4]
        self.PS, self.PO, self.PZ = c.psum[5:8]

    def sync(self, sync, rounds):
        sync.sem_inc(self.x_turned, 1)
        sync.sem_inc(self.res_done, 1)
        sync.sem_inc(self.stored, 1)

        def load(k, m, last):
            sync.wait_ge(self.x_turned, m + 1)
            sync.wait_ge(self.res_done, m + 1)
            load_rows(sync, self.x1r, self.x1_d, k, last, True, self.x_in)
            load_rows(sync, self.xr, self.x, k, last, False, self.x_in)

        def store(k, m, last):
            sync.wait_ge(self.z_done, m + 1)
            sync.dma_start(rows(self.z_d, k), self.zr[:, :, :]).then_inc(self.out, 16)
            sync.wait_ge(self.h_done, m + 1)
            sync.dma_start(rows(self.h_d, k), self.hr[:, :, :]).then_inc(self.out, 16)
            sync.dma_start(rows(self.feat_d, k), self.fr[:, :, :]).then_inc(self.out, 16)
            sync.wait_ge(self.out, m * 48 + 48)
            sync.sem_inc(self.stored, 1)
        prefetched(sync, rounds, load, store)

    def pe(self, pe, k, m, last):
        c = self.c
        pe.wait_ge(self.x_in, m * 64 + 64)
        pe.wait_ge(self.f_pre, m + 1)
        for a in range(CB):
            mm = pe.transpose(self.PT[:, a * P:(a + 1) * P], self.x1r[:, a, :], c.ident[:, :])
        mm.then_inc(self.x_turned, 1)
        pe.wait_ge(self.xT_done, m + 1)
        pe.matmul(self.PS[:, :], c.SL[1][:, :], self.xT[:, :], start=True, stop=True).then_inc(self.selfed, 1)
        pe.wait_ge(self.y_act, m + 1)
        for a in range(CB):
            mm = pe.transpose(self.PO[:, a * P:(a + 1) * P], self.yT[:, a * P:(a + 1) * P], c.ident[:, :])
        mm.then_inc(self.y_turned, 1)
        pe.wait_ge(self.z_done, m + 1)
        for a in range(CB):
            mm = pe.transpose(self.PZ[:, a * P:(a + 1) * P], self.zr[:, a, :], c.ident[:, :])
        mm.then_inc(self.z_turned, 1)
        pe.wait_ge(self.zT_done, m + 1)
        for a in range(CB):
            mm = pe.matmul(self.PF[:, a * D:(a + 1) * D], self.zT[:, a * P:(a + 1) * P], c.GW[0][:, :],
                           start=True, stop=True)
        mm.then_inc(self.f_mm, 1)

    def start_act(self, act):
        pass

    def act(self, act, k, m, last):
        act.wait_ge(self.x_turned, m + 2)
        act.copy(self.xT[:, :], self.PT[:, :]).then_inc(self.xT_done, 1)
        act.wait_ge(self.pre_done, m + 1)
        act.activation(self.yT[:, :], self.pre[:, :], ACT.Relu, bias=self.c.B[1][:, 0:1]).then_inc(self.y_act, 1)
        act.wait_ge(self.var_done, m + 1)
        act.activation(self.sd[:, 0, :], self.mv[:, :, 1], ACT.Sqrt, bias=self.c.eps[:, 0:1]).then_inc(self.sd_done, 1)
        act.wait_ge(self.z_turned, m + 1)
        act.copy(self.zT[:, :], self.PZ[:, :]).then_inc(self.zT_done, 1)
        act.wait_ge(self.f_pre, m + 2)
        act.wait_ge(self.stored, m + 1)
        act.activation(self.fr[:, :, :], self.fp[:, :, :], ACT.Relu).then_inc(self.f_done, 1)

    def end_act(self, act):
        pass

    def start_dve(self, dve):
        dve.sem_inc(self.f_pre, 1)

    def dve(self, dve, k, m, last):
        c = self.c
        dve.wait_ge(self.selfed, m + 1)
        dve.tensor_tensor(self.pre[:, :], self.PS[:, :], c.acc[:, bass.ds(k * CH, CH)], ALU.add
                          ).then_inc(self.pre_done, 1)
        dve.wait_ge(self.y_turned, m + 1)
        dve.wait_ge(self.x_in, m * 64 + 64)
        dve.tensor_tensor(self.rr[:, :, :], blocks(self.PO[:, :]), self.xr[:, :, :], ALU.add).then_inc(self.res_done, 1)
        dve.wait_ge(self.res_done, m + 2)
        ch = Chain(dve, self.steps, m * 5)
        stats(dve, ch, c.passed, self.rr, self.st, self.mv)
        dve.sem_inc(self.var_done, 1)
        dve.wait_ge(self.sd_done, m + 1)
        ch.then(dve.reciprocal(self.sd[:, 1, :], self.sd[:, 0, :]))
        dve.wait_ge(self.stored, m + 1)
        normed(dve, ch, self.rr, self.mv, self.sd[:, 1], self.zr)
        dve.sem_inc(self.z_done, 1)
        dve.wait_ge(self.f_mm, m + 1)
        dve.tensor_tensor(self.fp[:, :, :], blocks(self.PF[:, :]), c.GB[0][:, :].unsqueeze(1).broadcast_to([P, CB, D]),
                          ALU.add).then_inc(self.f_pre, 1)
        dve.wait_ge(self.f_done, m + 1)
        ch.then(dve.tensor_tensor(self.hr[:, :, :], self.fr[:, :, :], bc_last(c.dinv[:, bass.ds(k * CB, CB)], D),
                                  ALU.mult))
        dve.sem_inc(self.h_done, 1)
        assert ch.n == 5

    def end_dve(self, dve):
        pass


class Tail3:

    def __init__(self, nc, ctx, c, z_d, feat_d, out):
        def sb(name, shape):
            return ctx.enter_context(nc.sbuf_tensor(f"d3_{name}", shape, F32))

        def sem(name):
            return ctx.enter_context(nc.semaphore(f"d3_{name}"))

        self.c, self.z_d, self.feat_d, self.result = c, z_d, feat_d, out
        self.fr, self.zr, self.ag, self.ur, self.rr, self.r2, self.o = (
            sb(n, [P, CB, D]) for n in ("fr", "zr", "ag", "ur", "rr", "r2", "o"))
        self.aT, self.uT = sb("aT", [P, CH]), sb("uT", [P, CH])
        self.st, self.mv, self.sd = sb("st", [P, CB, 6]), sb("mv", [P, CB, 2]), sb("sd", [P, 2, CB])
        (self.in_, self.whole, self.aT_done, self.a_turned, self.u_done, self.u_turned, self.uT_done, self.v_mm,
         self.v_done, self.var_done, self.sd_done, self.o_done, self.out, self.stored, self.steps) = (
            sem(n) for n in ("in", "whole", "aT_done", "a_turned", "u_done", "u_turned", "uT_done", "v_mm", "v_done",
                             "var_done", "sd_done", "o_done", "out", "stored", "steps"))
        self.PA, self.PU, self.PV = c.psum[2:5]

    def sync(self, sync, rounds):
        sync.sem_inc(self.v_done, 1)
        sync.sem_inc(self.stored, 1)

        def load(k, m, last):
            sync.wait_ge(self.v_done, m + 1)
            load_rows(sync, self.fr, self.feat_d, k, last, True, self.in_)
            load_rows(sync, self.zr, self.z_d, k, last, True, self.in_)

        def store(k, m, last):
            sync.wait_ge(self.o_done, m + 1)
            if last:
                whole = N - LASTN + P
                sync.dma_start(self.result[N - LASTN:whole, :], self.o[:, 0, :]).then_inc(self.out, 16)
                sync.dma_start(self.result[whole:N, :], self.o[0:N - whole, 1, :]).then_inc(self.out, 16)
            else:
                for a in range(2):
                    sync.dma_start(rows(self.result, k)[:, 2 * a:2 * a + 2, :], self.o[:, 2 * a:2 * a + 2, :]
                                   ).then_inc(self.out, 16)
            sync.wait_ge(self.out, m * 32 + 32)
            sync.sem_inc(self.stored, 1)
        prefetched(sync, rounds, load, store)

    def pe(self, pe, k, m, last):
        c = self.c
        pe.wait_ge(self.aT_done, m + 1)
        for a in range(CB):
            mm = pe.transpose(self.PA[:, a * P:(a + 1) * P], self.aT[:, a * P:(a + 1) * P], c.ident[:, :])
        mm.then_inc(self.a_turned, 1)
        pe.wait_ge(self.u_done, m + 1)
        for a in range(CB):
            mm = pe.transpose(self.PU[:, a * P:(a + 1) * P], self.ur[:, a, :], c.ident[:, :])
        mm.then_inc(self.u_turned, 1)
        pe.wait_ge(self.uT_done, m + 1)
        pe.wait_ge(self.v_done, m + 1)
        for a in range(CB):
            mm = pe.matmul(self.PV[:, a * D:(a + 1) * D], self.uT[:, a * P:(a + 1) * P], c.GW[1][:, :],
                           start=True, stop=True)
        mm.then_inc(self.v_mm, 1)

    def start_act(self, act):
        pass

    def act(self, act, k, m, last):
        act.wait_ge(self.whole, m + 1)
        act.copy(self.aT[:, :], self.c.acc[:, bass.ds(k * CH, CH)]).then_inc(self.aT_done, 1)
        act.wait_ge(self.u_turned, m + 1)
        act.copy(self.uT[:, :], self.PU[:, :]).then_inc(self.uT_done, 1)
        act.wait_ge(self.var_done, m + 1)
        act.activation(self.sd[:, 0, :], self.mv[:, :, 1], ACT.Sqrt, bias=self.c.eps[:, 0:1]).then_inc(self.sd_done, 1)

    def end_act(self, act):
        pass

    def start_dve(self, dve):
        pass

    def dve(self, dve, k, m, last):
        c = self.c
        dve.sem_inc(self.whole, 1)
        ch = Chain(dve, self.steps, m * 6)
        dve.wait_ge(self.a_turned, m + 1)
        ch.then(dve.tensor_tensor(self.ag[:, :, :], blocks(self.PA[:, :]), bc_last(c.dinv[:, bass.ds(k * CB, CB)], D),
                                  ALU.mult))
        dve.wait_ge(self.in_, m * 64 + 64)
        dve.tensor_tensor(self.ur[:, :, :], self.fr[:, :, :], self.ag[:, :, :], ALU.subtract).then_inc(self.u_done, 1)
        dve.wait_ge(self.v_mm, m + 1)
        dve.tensor_tensor(self.rr[:, :, :], blocks(self.PV[:, :]), self.zr[:, :, :], ALU.add).then_inc(self.v_done, 1)
        dve.wait_ge(self.v_done, m + 2)
        ch.then(dve.tensor_tensor(self.r2[:, :, :], self.rr[:, :, :],
                                  c.GB[1][:, :].unsqueeze(1).broadcast_to([P, CB, D]), ALU.add))
        stats(dve, ch, c.passed, self.r2, self.st, self.mv)
        dve.sem_inc(self.var_done, 1)
        dve.wait_ge(self.sd_done, m + 1)
        ch.then(dve.reciprocal(self.sd[:, 1, :], self.sd[:, 0, :]))
        dve.wait_ge(self.stored, m + 1)
        normed(dve, ch, self.r2, self.mv, self.sd[:, 1], self.o)
        dve.sem_inc(self.o_done, 1)
        assert ch.n == 6

    def end_dve(self, dve):
        pass


def stats(dve, ch, passed, r, st, mv):
    for a in range(CB):
        ins = dve.bn_stats(st[:, a, :], r[:, a, :])
    ch.then(ins)
    gate(dve, passed)
    for a in range(CB):
        ins = dve.bn_aggr(mv[:, a, :], st[:, a, :])
    ch.then(ins)


def normed(dve, ch, r, mv, rstd, z):
    for a in range(CB):
        ins = dve.tensor_scalar(z[:, a, :], r[:, a, :], mv[:, a, 0:1], rstd[:, a:a + 1], ALU.subtract, ALU.mult)
    ch.then(ins)


_INS = ['x', 'src', 'dst', 'edge_type_8', 'L0_gnn_w1', 'L0_gnn_sl1', 'L0_gnn_b1', 'L0_gnn_w2', 'L0_gnn_sl2',
        'L0_gnn_b2', 'L1_gnn_W1', 'L1_gnn_b1', 'L1_gnn_W2', 'L1_gnn_b2']


def kernel(**inputs):
    import numpy as _np
    import concourse.bacc as _bacc
    from concourse import mybir as _mybir
    from concourse.bass_utils import run_bass_kernel_spmd as _run

    nc = _bacc.Bacc("TRN2", target_bir_lowering=False, num_devices=1)
    arrays, args = {}, []
    for name in _INS:
        a = _np.ascontiguousarray(inputs[name])
        arrays[f"in_{name}_dram"] = a
        args.append(nc.dram_tensor(f"in_{name}_dram", a.shape, _mybir.dt.from_np(a.dtype), kind="ExternalInput").ap())
    o = nc.dram_tensor("out_0_dram", (N, D), _mybir.dt.float32, kind="ExternalOutput").ap()
    build(nc, *args, o)
    r = _run(nc, [arrays], core_ids=[0])
    return r.results[0]["out_0_dram"]
```

```python
import concourse.bass as bass
from concourse import mybir
from contextlib import ExitStack

F32 = mybir.dt.float32
I32 = mybir.dt.int32
BF16 = mybir.dt.bfloat16
ALU = mybir.AluOpType
ACT = mybir.ActivationFunctionType
AX = mybir.AxisListType

P = 128
D = 128
N = 12500
E = 212500
NREL = 8
EPS = 1e-5

KG = 7
GN = 64
TN = 16
TK = TN * NREL
RING = 4
BUFS = 2
UN = RING * KG
TB = 119
NTB = 14
NT = TB * NTB
NG = NT // KG
IT = NG // RING
TILES = -(-E // P)
FULL = [KG] * RING
LEFT = [min(KG, TILES - g * KG) for g in range(IT * RING, NG)]
assert NT % KG == 0 and min(LEFT) > 0 and RING % BUFS == 0 and NG % BUFS == 0 and len(LEFT) == BUFS

CH = 512
CB = CH // P
NCH = -(-N // CH)
LASTN = N - (NCH - 1) * CH
LASTB = -(-LASTN // P)
NB = (NCH - 1) * CB + LASTB
NPAD = NB * P
assert LASTB == 2
ACC = NPAD + GN


class Chain:

    def __init__(self, eng, sem, base):
        self.eng, self.sem, self.base, self.n = eng, sem, base, 0

    def then(self, ins):
        ins.then_inc(self.sem, 1)
        self.n += 1
        self.eng.wait_ge(self.sem, self.base + self.n)


def gate(eng, passed):
    eng.sem_inc(passed, 1)


def bc_last(ap, n):
    return ap.unsqueeze(len(ap.shape)).broadcast_to([*ap.shape, n])


def build(nc, x, src, dst, rel, w1, sl1, b1, w2, sl2, b2, gw1, gb1, gw2, gb2, out):
    with ExitStack() as top:
        def sb(name, shape, dt=F32):
            return top.enter_context(nc.sbuf_tensor(name, shape, dt))

        def scratch(name, *shape):
            return nc.dram_tensor(name, shape, F32, kind="Internal").ap()

        tile_lo_d, tile_hi_d = scratch("tile_lo_d", NT), scratch("tile_hi_d", NT)
        x1_d, z_d, feat_d, h_d = (scratch(n, NPAD, D) for n in ("x1_d", "z_d", "feat_d", "h_d"))

        c = Shared()
        c.W = [sb("w1s", [P, NREL, D]), sb("w2s", [P, NREL, D])]
        c.SL = [sb("sl1s", [P, D]), sb("sl2s", [P, D])]
        c.B = [sb("b1s", [P, 1]), sb("b2s", [P, 1])]
        c.GW = [sb("gw1s", [P, D]), sb("gw2s", [P, D])]
        c.GB = [sb("gb1s", [P, D]), sb("gb2s", [P, D])]
        c.ident = sb("ident", [P, P])
        c.iota = sb("iota", [P, TK])
        c.zeros_bf = sb("zeros_bf", [P, P], BF16)
        c.zeros = c.zeros_bf[:, 0:1].broadcast_to([P, CH])
        c.ones_bf = sb("ones_bf", [P, 1], BF16)
        c.one = sb("one", [1, 1])
        c.eps = sb("eps", [P, 1])
        c.src_i = sb("src_i", [P, NT + UN], I32)
        c.node = sb("node", [P, NT])
        c.relf = sb("relf", [P, NT])
        c.lo_b = sb("lo_b", [P, NT])
        c.glo = sb("glo", [P, NG])
        c.key = sb("key", [P, NT])
        c.gs = sb("gs", [P, NG])
        c.off_i = sb("off_i", [1, NG, KG], I32)
        c.gs_i = sb("gs_i", [1, NG], I32)
        c.gs8 = sb("gs8", [1, NG])
        c.step_t, c.step_g, c.carry = sb("step_t", [P, 1]), sb("step_g", [P, 1]), sb("carry", [P, 1])
        c.t = [sb("t1", [P, NT]), sb("t2", [P, NT])]
        c.deg = sb("deg", [P, NB])
        c.dinv = sb("dinv", [P, NB])
        c.acc = sb("acc", [P, ACC])
        c.rounds_i = sb("rounds_i", [1, 2], I32)
        c.ends_i = sb("ends_i", [1, 1 + NCH], I32)
        c.passed = top.enter_context(nc.semaphore("passed"))
        c.psum = [top.enter_context(nc.psum_tensor(f"bank{i}", [P, CH], F32)) for i in range(8)]

        loads = [(c.W[0], w1.rearrange("r i o -> i r o")), (c.W[1], w2.rearrange("r i o -> i r o")),
                 (c.SL[0], sl1), (c.SL[1], sl2), (c.GW[0], gw1), (c.GW[1], gw2),
                 (c.B[0], b1.rearrange("(p a) -> p a", a=1)), (c.B[1], b2.rearrange("(p a) -> p a", a=1)),
                 (c.GB[0], gb1.partition_broadcast(P)), (c.GB[1], gb2.partition_broadcast(P))]
        with ExitStack() as ctx:
            cnt = ctx.enter_context(nc.sbuf_tensor("cnt", [1, ACC], F32))
            prologue = Prologue(nc, ctx, c, (dst, src, rel), loads, tile_lo_d, tile_hi_d)
            tail = Tail1(nc, ctx, c, x, x1_d, cnt)
            relational_sum(nc, ctx, c, "r1", x, c.W[0], cnt, tail, prologue)
        with ExitStack() as ctx:
            tail = Tail2(nc, ctx, c, x, x1_d, z_d, feat_d, h_d)
            relational_sum(nc, ctx, c, "r2", x1_d, c.W[1], None, tail, None)
        with ExitStack() as ctx:
            tail = Tail3(nc, ctx, c, z_d, feat_d, out)
            plain_sum(nc, ctx, c, h_d, tail)


class Shared:
    pass


class Prologue:

    def __init__(self, nc, ctx, c, edges, loads, tile_lo_d, tile_hi_d):
        def sb(name, shape, dt=F32):
            return ctx.enter_context(nc.sbuf_tensor(f"p_{name}", shape, dt))

        def sem(name):
            return ctx.enter_context(nc.semaphore(f"p_{name}"))

        self.nc, self.c, self.edges, self.loads = nc, c, edges, loads
        self.tile_lo_d, self.tile_hi_d = tile_lo_d, tile_hi_d
        w = NTB * P
        part = [c.acc[0:TB, i * w:(i + 1) * w] for i in range(6)]
        by_block = lambda ap: ap.rearrange("p (j e) -> p j e", e=P)
        self.raw = [by_block(part[i].bitcast(I32)) for i in range(3)]
        self.rawf = [by_block(part[3 + i]) for i in range(3)]
        assert 6 * w <= ACC and NG % 2 == 0
        self.tlo, self.thi, self.tspan = sb("tlo", [TB, NTB]), sb("thi", [TB, NTB]), sb("tspan", [TB, NTB])
        self.pairs = NG // 2
        self.glo7, self.ghi7 = sb("glo7", [self.pairs, 2, KG]), sb("ghi7", [self.pairs, 2, KG])
        self.glo2, self.ghi2 = sb("glo2", [self.pairs, 2]), sb("ghi2", [self.pairs, 2])
        self.widest = sb("widest", [TB, 2])
        assert self.pairs == TB
        self.sp, self.spi = sb("sp", [1, 8]), sb("spi", [1, 2], I32)
        self.ilo, self.done, self.ends = sb("ilo", [P, IT]), sb("done", [P, IT]), sb("ends", [P, 1])
        self.count, self.above = sb("count", [P, IT]), sb("above", [P, 1])
        (self.padded, self.consts, self.ident0, self.weights_in, self.dst_f, self.other_f, self.tiles, self.turned,
         self.placed, self.src_placed, self.tile_out, self.group_in, self.lo_in, self.steps, self.widest_ready,
         self.turned2, self.zeroed, self.ready) = (
            sem(n) for n in ("padded", "consts", "ident0", "weights_in", "dst_f", "other_f", "tiles", "turned",
                             "placed", "src_placed", "tile_out", "group_in", "lo_in", "steps", "widest_ready",
                             "turned2", "zeroed", "ready"))
        self.raw_in = [sem(f"raw_in{n}") for n in range(3)]

    CONSTS = 12
    BANKS = -(-NTB // 4)

    def sync(self, sync):
        full = E // P
        before = (NTB - 1) * TB
        sync.wait_ge(self.padded, 3)
        for a, r, done in zip(self.edges, self.raw, self.raw_in):
            sync.dma_start(r[:, 0:NTB - 1, :], a[0:before * P].rearrange("(j p e) -> p j e", j=NTB - 1, p=TB)
                           ).then_inc(done, 16)
            sync.dma_start(r[0:full - before, NTB - 1, :], a[before * P:full * P].rearrange("(p e) -> p e", e=P)
                           ).then_inc(done, 16)
            sync.dma_start(r[full - before:full - before + 1, NTB - 1, 0:E - full * P],
                           a[full * P:E].rearrange("(p e) -> p e", p=1)).then_inc(done, 16)
        sync.wait_ge(self.tiles, 2)
        for to, of in ((self.tile_lo_d, self.tlo), (self.tile_hi_d, self.thi)):
            sync.dma_start(to.rearrange("(j p) -> p j", p=TB), of[:, :], allow_slow_non_contiguous=True
                           ).then_inc(self.tile_out, 16)
        sync.wait_ge(self.tile_out, 32)
        sync.dma_start(self.c.lo_b[:, :], self.tile_lo_d.partition_broadcast(P)).then_inc(self.lo_in, 16)
        for to, of in ((self.glo7, self.tile_lo_d), (self.ghi7, self.tile_hi_d)):
            sync.dma_start(to[:, :, :], of.rearrange("(p g k) -> p g k", g=2, k=KG)).then_inc(self.group_in, 16)
        for to, of in self.loads:
            sync.dma_start(to[:], of).then_inc(self.weights_in, 16)
        sync.wait_ge(self.ready, 1)

    def pool(self, pool):
        c = self.c
        pool.memset(c.ident[:, :], 0.0).then_inc(self.ident0, 1)
        pool.wait_ge(self.ident0, 1)
        pool.affine_select(out=c.ident[:, :], in_=c.ident[:, :], compare_op=ALU.not_equal, fill=1.0, base=0,
                           pattern=[[-1, P]], channel_multiplier=1).then_inc(self.consts, 1)
        pool.iota(self.count[:, :], [[1, IT]], base=1, channel_multiplier=0,
                  allow_small_or_imprecise_dtypes=True).then_inc(self.consts, 1)
        pool.iota(self.above[:, :], [[1, 1]], base=CH, channel_multiplier=CH,
                  allow_small_or_imprecise_dtypes=True).then_inc(self.consts, 1)
        pool.iota(c.iota[:, :], [[1, TK]], base=0, channel_multiplier=0,
                  allow_small_or_imprecise_dtypes=True).then_inc(self.consts, 1)

    def pe(self, pe):
        c = self.c
        pe.wait_ge(self.consts, self.CONSTS)
        n = 0
        for a in range(3):
            if a == 0:
                pe.wait_ge(self.dst_f, 1)
            else:
                pe.wait_ge(self.other_f, a)
            for j0 in range(0, NTB, 4):
                if n >= 8:
                    pe.wait_ge(self.placed, n - 7)
                for j in range(j0, min(j0 + 4, NTB)):
                    mm = pe.transpose(c.psum[n % 8][:, (j - j0) * TB:(j - j0 + 1) * TB], self.rawf[a][:, j, :],
                                      c.ident[0:TB, 0:TB])
                mm.then_inc(self.turned, 1)
                n += 1
        assert n == 3 * self.BANKS and 2 * self.BANKS == 8
        pe.wait_ge(self.src_placed, self.BANKS)
        pe.wait_ge(self.widest_ready, 1)
        for a in range(2):
            mm = pe.transpose(c.psum[6][0:1, a * P:a * P + TB], self.widest[:, a:a + 1], c.ident[0:TB, 0:TB])
        mm.then_inc(self.turned2, 1)
        pe.wait_ge(self.widest_ready, 2)
        pe.transpose(c.psum[7][0:1, 0:P], self.ends[:, 0:1], c.ident[:, :]).then_inc(self.turned2, 1)
        pe.wait_ge(self.ready, 1)

    def place(self, eng_copy, to, a, m):
        n = min(4, NTB - 4 * m) * TB
        return eng_copy(to[:, 4 * m * TB:4 * m * TB + n], self.c.psum[(a * self.BANKS + m) % 8][:, 0:n])

    def act(self, act, first, cnt):
        c = self.c
        act.wait_ge(self.raw_in[1], 48)
        act.copy(self.rawf[1], self.raw[1]).then_inc(self.other_f, 1)
        act.wait_ge(self.raw_in[2], 48)
        act.copy(self.rawf[2], self.raw[2]).then_inc(self.other_f, 1)
        for m in range(self.BANKS):
            act.wait_ge(self.turned, self.BANKS + m + 1)
            self.place(act.copy, c.src_i, 1, m).then_inc(self.src_placed, 1)
        act.wait_ge(self.src_placed, 1)
        first(act)
        act.wait_ge(self.consts, self.CONSTS)
        zero(act, c, cnt[:, :]).then_inc(self.zeroed, 1)
        act.wait_ge(self.turned, 3 * self.BANKS)
        act.wait_ge(self.tiles, 2)
        zero(act, c, c.acc[:, :]).then_inc(self.zeroed, 1)
        act.wait_ge(self.ready, 1)
        act.wait_ge(self.src_placed, self.BANKS)

    def dve(self, dve):
        c = self.c
        for r, pad in zip(self.raw, (N, 0, 0)):
            dve.memset(r[:, NTB - 1, :], pad).then_inc(self.padded, 1)
        for ap, value in ((c.zeros_bf[:, :], 0.0), (c.ones_bf[:, :], 1.0), (c.one[:, :], 1.0), (c.eps[:, :], EPS),
                          (c.src_i[:, NT:], 0), (c.ends_i[:, 0:1], 0), (c.step_t[:, :], 0.0), (c.step_g[:, :], 0.0)):
            dve.memset(ap, value).then_inc(self.consts, 1)
        dve.wait_ge(self.raw_in[0], 48)
        dve.tensor_copy(self.rawf[0], self.raw[0]).then_inc(self.dst_f, 1)
        dve.wait_ge(self.dst_f, 1)
        dve.tensor_reduce(self.tlo[:, :], self.rawf[0], AX.X, ALU.min).then_inc(self.tiles, 1)
        dve.tensor_reduce(self.thi[:, :], self.rawf[0], AX.X, ALU.max).then_inc(self.tiles, 1)
        for a, to in ((0, c.node), (2, c.relf)):
            for m in range(self.BANKS):
                dve.wait_ge(self.turned, a * self.BANKS + m + 1)
                self.place(dve.tensor_copy, to, a, m).then_inc(self.placed, 1)
        ch = Chain(dve, self.steps, 0)
        dve.wait_ge(self.tiles, 2)
        ch.then(dve.tensor_tensor(self.tspan[:, :], self.thi[:, :], self.tlo[:, :], ALU.subtract))
        ch.then(dve.tensor_reduce(self.widest[:, 0:1], self.tspan[:, :], AX.X, ALU.max))
        dve.wait_ge(self.lo_in, 16)
        ch.then(dve.tensor_reduce(c.glo[:, :], by_group(c.lo_b), AX.X, ALU.min))
        dve.wait_ge(self.group_in, 32)
        ch.then(dve.tensor_reduce(self.glo2[:, :], self.glo7[:, :, :], AX.X, ALU.min))
        ch.then(dve.tensor_reduce(self.ghi2[:, :], self.ghi7[:, :, :], AX.X, ALU.max))
        ch.then(dve.tensor_tensor(self.ghi2[:, :], self.ghi2[:, :], self.glo2[:, :], ALU.subtract))
        dve.tensor_reduce(self.widest[:, 1:2], self.ghi2[:, :], AX.X, ALU.max).then_inc(self.widest_ready, 1)
        ch.then(dve.tensor_reduce(self.ilo[:, :], c.glo[:, 0:IT * RING].rearrange("p (i h) -> p i h", h=RING), AX.X,
                                  ALU.min))
        dve.wait_ge(self.consts, self.CONSTS)
        ch.then(dve.scalar_tensor_tensor(self.done[:, :], self.ilo[:, :], self.above[:, 0:1], self.count[:, :],
                                         ALU.is_lt, ALU.mult))
        dve.tensor_reduce(self.ends[:, :], self.done[:, :], AX.X, ALU.max).then_inc(self.widest_ready, 1)
        dve.wait_ge(self.placed, 2 * self.BANKS)
        window_columns(dve, c, ch, c.glo, c.lo_b, c.t[1])
        ch.then(dve.scalar_tensor_tensor(c.key[:, :], c.t[1][:, :], float(NREL), c.relf[:, :], ALU.mult, ALU.add))
        sp, spi = self.sp, self.spi
        dve.wait_ge(self.turned2, 2)
        dve.tensor_copy(c.ends_i[0:1, 1:1 + NCH], c.psum[7][0:1, 0:NCH]).then_inc(self.consts, 1)
        ch.then(dve.tensor_reduce(sp[:, 0:2], c.psum[6][0:1, 0:2 * P].rearrange("p (a t) -> p a t", t=P)[:, :, 0:TB],
                                  AX.X, ALU.max))
        ch.then(dve.tensor_copy(spi[:, 0:1], sp[:, 1:2]))
        ch.then(dve.tensor_scalar(spi[:, 1:2], spi[:, 0:1], GN.bit_length() - 1, None, ALU.arith_shift_right))
        ch.then(dve.tensor_copy(sp[:, 2:3], spi[:, 1:2]))
        ch.then(dve.tensor_scalar(sp[:, 3:4], sp[:, 2:3], 1.0, None, ALU.add))
        ch.then(dve.tensor_scalar(sp[:, 4:5], sp[:, 0:1], float(TN), None, ALU.is_ge))
        ch.then(dve.tensor_scalar(sp[:, 5:6], sp[:, 1:2], float(GN), None, ALU.is_ge))
        ch.then(dve.tensor_tensor(sp[:, 4:5], sp[:, 4:5], sp[:, 5:6], ALU.max))
        ch.then(dve.tensor_scalar(sp[:, 5:6], sp[:, 3:4], float(GN // TN), -1.0, ALU.mult, ALU.add))
        ch.then(dve.tensor_tensor(sp[:, 5:6], sp[:, 5:6], sp[:, 4:5], ALU.mult))
        ch.then(dve.tensor_scalar(sp[:, 2:3], sp[:, 5:6], 1.0, None, ALU.add))
        ch.then(dve.tensor_reduce(sp[:, 6:7], c.glo[0:1, IT * RING:], AX.X, ALU.min))
        ch.then(dve.tensor_scalar(sp[:, 6:7], sp[:, 6:7], float((NCH - 2) * CH), None, ALU.is_lt))
        ch.then(dve.tensor_scalar(c.rounds_i[:, :], sp[0:1, 2:4], sp[0:1, 6:7], None, ALU.add))
        dve.wait_ge(self.consts, self.CONSTS + 1)
        dve.wait_ge(self.weights_in, 16 * len(self.loads))
        dve.wait_ge(self.src_placed, self.BANKS)
        dve.sem_inc(self.ready, 1)


def by_group(a):
    return a[:, :].rearrange("p (g k) -> p g k", k=KG)


def zero(act, c, ap):
    return act.copy(ap, c.zeros_bf[0:ap.shape[0], 0:1].broadcast_to([*ap.shape]))


def window_columns(dve, c, ch, gs, start, t2):
    gsb = bc_last(gs[:, :], KG)
    ch.then(dve.scalar_tensor_tensor(by_group(t2), gsb, float(GN - TN), by_group(start), ALU.add, ALU.min))
    ch.then(dve.tensor_scalar(c.gs8[:, :], gs[0:1, :], float(NREL), None, ALU.mult))
    ch.then(dve.scalar_tensor_tensor(c.off_i[:, :, :], by_group(t2)[0:1, :, :], float(NREL), bc_last(c.gs8[:, :], KG),
                                     ALU.mult, ALU.subtract))
    ch.then(dve.tensor_scalar(c.gs_i[:, :], gs[0:1, :], float(NPAD), None, ALU.min))
    ch.then(dve.tensor_tensor(t2[:, :], c.node[:, :], t2[:, :], ALU.subtract))


def windows(dve, c, ch):
    t1, t2 = c.t
    n = ch.n
    ch.then(dve.tensor_scalar(c.gs[:, :], c.glo[:, :], c.step_g[:, 0:1], None, ALU.add))
    ch.then(dve.tensor_tensor(by_group(t1), by_group(c.lo_b), bc_last(c.gs[:, :], KG), ALU.max))
    ch.then(dve.tensor_scalar(t1[:, :], t1[:, :], c.step_t[:, 0:1], None, ALU.add))
    window_columns(dve, c, ch, c.gs, t1, t2)
    ch.then(dve.tensor_tensor(t1[:, :], c.node[:, :], t1[:, :], ALU.is_ge))
    ch.then(dve.scalar_tensor_tensor(t2[:, :], t2[:, :], float(NREL), c.relf[:, :], ALU.mult, ALU.add))
    ch.then(dve.scalar_tensor_tensor(t2[:, :], t2[:, :], 1.0, t1[:, :], ALU.add, ALU.mult))
    ch.then(dve.tensor_scalar(c.key[:, :], t2[:, :], -1.0, None, ALU.add))
    ch.then(dve.tensor_scalar(c.step_t[:, :], c.step_t[:, :], float(TN), None, ALU.add))
    ch.then(dve.tensor_scalar(c.carry[:, :], c.step_t[:, :], float(GN), float(GN), ALU.is_ge, ALU.mult))
    ch.then(dve.tensor_tensor(c.step_t[:, :], c.step_t[:, :], c.carry[:, :], ALU.subtract))
    ch.then(dve.tensor_tensor(c.step_g[:, :], c.step_g[:, :], c.carry[:, :], ALU.add))
    assert ch.n - n == WINDOW_STEPS


WINDOW_STEPS = 16


class Chunk:

    def __init__(self, q, k, m, s=0, b=CB):
        self.k, self.m, self.s, self.b, self.n = k, m, s, b, b * P
        self.last = s == 1
        self.i = q if self.last else q * (NCH - 1) + k
        self.free = m + 1 - s
        self.cols = bass.ds(k * CH, self.n)
        self.blocks = bass.ds(k * CB, b)


def last_two(q):
    m = q * NCH + (NCH - 2)
    return [Chunk(q, NCH - 2, m), Chunk(q, NCH - 1, m + 1, 1, LASTB)]


def by_chunk(eng, c, q, iteration, early, late):
    def reach(k):
        since = eng.value_load(c.ends_i[0:1, bass.ds(k, 1)], min_val=0, max_val=IT)
        until = eng.value_load(c.ends_i[0:1, bass.ds(k + 1, 1)], min_val=0, max_val=IT)
        with eng.If(since < until):
            with eng.Fori(since, until) as i:
                iteration(i, FULL)
        eng.end_ifs()

    early(eng, [Chunk(q, 0, q * NCH)])
    with eng.Fori(0, NCH - 2) as k:
        m = eng.snap(q * NCH + k)
        reach(k)
        late(eng, [Chunk(q, k, m)], [Chunk(q, k + 1, m + 1)])
    two = last_two(q)
    early(eng, two[1:])
    reach(NCH - 2)
    reach(NCH - 1)
    iteration(IT, LEFT)
    late(eng, two, [])


def rounds_of(eng, c, which, most):
    return eng.value_load(c.rounds_i[0:1, which:which + 1], min_val=1, max_val=most)


class Gathers:

    def __init__(self, nc, ctx, c, tag, table, which, most):
        def sem(name):
            return ctx.enter_context(nc.semaphore(f"{tag}_{name}"))

        self.c, self.table, self.which, self.most = c, table, which, most
        self.rows = ctx.enter_context(nc.sbuf_tensor(f"{tag}_rows", [P, UN, D], F32))
        self.idx = ctx.enter_context(nc.sbuf_tensor(f"{tag}_idx", [P, UN], I32))
        self.landed = [sem(f"landed{h}") for h in range(RING)]
        assert [s.num - self.landed[0].num for s in self.landed] == list(range(RING))
        self.cleared = sem("cleared")
        self.idx_ready = sem("idx_ready")
        self.summed = sem("summed")

    def start(self, pe):
        pe.sem_inc(self.summed, RING)

    def first(self, act):
        for h in range(RING):
            act.copy(self.idx[:, h * KG:(h + 1) * KG], self.c.src_i[:, h * KG:(h + 1) * KG]).then_inc(self.idx_ready, 1)

    def take(self, act, h, q, i):
        act.wait_ge(self.idx_ready, (q * (IT + 1) + i - 1) * RING + h + 1)
        act.wait_ge(self.summed, q * NG + (i * RING + h + 1))
        act.copy(self.idx[:, h * KG:(h + 1) * KG], self.c.src_i[:, bass.ds(i * UN + h * KG, KG)]
                 ).then_inc(self.idx_ready, 1)

    def again(self, act, q):
        act.wait_ge(self.summed, q * NG + (NG + RING))
        for h in range(RING):
            self.take(act, h, q + 1, 0)

    def run(self, pool, ready):
        def iteration(q, i, tiles):
            for h in range(len(tiles)):
                pool.wait_ge(self.idx_ready, (q * (IT + 1) + i) * RING + h + 1)
                pool.wait_ge(self.summed, q * NG + (i * RING + h + 1))
                gate(pool, self.c.passed)
                for s in range(h * KG, h * KG + tiles[h]):
                    pool.indirect_dma_start(
                        out=self.rows[:, s, :], out_offset=None, in_=self.table[:, :],
                        in_offset=bass.IndirectOffsetOnAxis(ap=self.idx[:, s:s + 1], axis=0)
                    ).then_inc(self.landed[h], 16)

        def one_round(q):
            with pool.Fori(0, IT) as i:
                iteration(q, i, FULL)
            iteration(q, IT, LEFT)

        pool.sem_inc(self.cleared, 1)
        one_round(0)
        if ready is not None:
            pool.wait_ge(ready, 1)
            gate(pool, self.c.passed)
        rounds = rounds_of(pool, self.c, self.which, self.most)
        with pool.If(rounds > 1):
            with pool.Fori(1, rounds) as q:
                pool.wait_ge(self.summed, q * NG + RING)
                gate(pool, self.c.passed)
                landed = range(self.landed[0].num, self.landed[0].num + RING)
                pool.dma_reset(landed)
                pool.sem_clear(landed)
                pool.sem_inc(self.cleared, 1)
                one_round(q)
        pool.end_ifs()

    def wait_rows(self, pe, h, i, tiles):
        pe.wait_ge(self.landed[h], (i * KG + tiles[h]) * 16)


def relational_sum(nc, ctx, c, tag, table, W, cnt, tail, prologue):
    def sb(name, shape, dt=F32):
        return ctx.enter_context(nc.sbuf_tensor(f"{tag}_{name}", shape, dt))

    def sem(name):
        return ctx.enter_context(nc.semaphore(f"{tag}_{name}"))

    most = 4 * (N // GN + 1) + 1
    g = Gathers(nc, ctx, c, tag, table, 0, most)
    summed = g.summed
    S = sb("S", [P, BUFS, KG, TK])
    agg = sb("agg", [P, BUFS, GN, NREL])
    dsum = sb("dsum", [1, GN])
    hot_ready = sem("hot_ready")
    agg_out = sem("agg_out")
    mixed = sem("mixed")
    added = sem("added")
    tables = sem("tables")
    steps, table_steps, setup = sem("steps"), sem("table_steps"), sem("setup")
    zeroed, zeros = (prologue.zeroed, 2) if prologue else (sem("zeroed"), 1)
    agg_ps, mix_ps, cnt_ps = c.psum[0:2], c.psum[2][:, 0:GN], c.psum[4:6]
    block = ctx.enter_context(nc.Block())

    @block.sync
    def _(sync):
        if prologue:
            prologue.sync(sync)
        tail.sync(sync, rounds_of(sync, c, 0, most))

    @block.scalar
    def _(act):
        if prologue:
            prologue.act(act, g.first, cnt)
        else:
            g.first(act)
            zero(act, c, c.acc[:, :]).then_inc(zeroed, 1)
        rounds = rounds_of(act, c, 0, most)
        with act.Fori(0, rounds) as q:
            def iteration(i, tiles):
                n = act.snap(q * NG + i * RING)
                for h in range(len(tiles)):
                    b = h % BUFS
                    act.wait_ge(summed, n + (h + 1 + RING))
                    act.wait_ge(mixed, n + (h + 1))
                    act.copy(agg[:, b, :, :], agg_ps[b][:, :].rearrange("p (n r) -> p n r", r=NREL)
                             ).then_inc(agg_out, 1)
                    if tiles is FULL:
                        g.take(act, h, q, i + 1)
            by_chunk(act, c, q, iteration, tail.act_early, tail.act_late)
            g.again(act, q)
        tail.end_act(act, rounds)

    @block.gpsimd
    def _(pool):
        if prologue:
            prologue.pool(pool)
        g.run(pool, prologue and prologue.ready)

    @block.tensor
    def _(pe):
        g.start(pe)
        pe.sem_inc(mixed, BUFS)
        if prologue:
            prologue.pe(pe)
        rounds = rounds_of(pe, c, 0, most)
        with pe.Fori(0, rounds) as q:
            pe.wait_ge(tables, q + 1)
            pe.wait_ge(g.cleared, q + 1)
            gate(pe, c.passed)

            def iteration(i, tiles):
                n = pe.snap(q * NG + i * RING)

                def mix(h):
                    b = h % BUFS
                    pe.wait_ge(agg_out, n + (h + 1 + BUFS))
                    pe.wait_ge(added, n + (h + BUFS))
                    for r in range(NREL):
                        mm = pe.matmul(mix_ps, W[:, r, :], agg[:, b, :, r],
                                       start=(r == 0), stop=(r == NREL - 1))
                    mm.then_inc(mixed, 1)

                for h in range(len(tiles)):
                    b = h % BUFS
                    _, offs = nc.values_load_multi_w_load_instructions(
                        c.off_i[0:1, bass.ds(i * RING + h, 1), :], engines=bass.OrderedEngineSet([pe.engine]),
                        min_val=0, max_val=(GN - TN) * NREL, skip_runtime_bounds_check_because="clamped on the chip")
                    pe.wait_ge(agg_out, n + (h + 1))
                    pe.matmul(agg_ps[b][:, :], c.zeros_bf[:, :], c.zeros, start=True, stop=False,
                              skip_group_check=True)
                    if cnt is not None:
                        pe.wait_ge(added, n + (h + 1))
                        pe.matmul(cnt_ps[b][0:1, :], c.zeros_bf[:, 0:1], c.zeros, start=True, stop=False,
                                  skip_group_check=True)
                    pe.wait_ge(hot_ready, n + (h + 1))
                    g.wait_rows(pe, h, i, tiles)
                    for k in range(tiles[h]):
                        mm = pe.matmul(agg_ps[b][:, bass.ds(offs[k], TK)], g.rows[:, h * KG + k, :], S[:, b, k, :],
                                       start=False, stop=(k == tiles[h] - 1), skip_group_check=True)
                        if cnt is not None:
                            mm = pe.matmul(cnt_ps[b][0:1, bass.ds(offs[k], TK)], c.ones_bf[:, :],
                                           S[:, b, k, :].bitcast(BF16)[:, 1:2 * TK:2],
                                           start=False, stop=(k == tiles[h] - 1), skip_group_check=True)
                    mm.then_inc(summed, 1)
                    if h > 0:
                        mix(h - 1)
                mix(len(tiles) - 1)
            by_chunk(pe, c, q, iteration, tail.pe_early, tail.pe_late)

    @block.vector
    def _(dve):
        dve.sem_inc(added, BUFS)
        dve.sem_inc(agg_out, BUFS)
        if prologue:
            prologue.dve(dve)
        tail.start_dve(dve)
        rounds = rounds_of(dve, c, 0, most)
        with dve.If(rounds > 1):
            dve.memset(c.step_t[:, :], 0.0).then_inc(setup, 1)
            dve.memset(c.step_g[:, :], 0.0).then_inc(setup, 1)
            dve.wait_ge(setup, 2)
            gate(dve, c.passed)
        dve.end_ifs()

        def one_hot(h, q, i):
            dve.wait_ge(summed, q * NG + (i * RING + (h + 1 - BUFS + RING)))
            dve.tensor_tensor(
                S[:, h % BUFS, :, :], c.iota[:, :].unsqueeze(1).broadcast_to([P, KG, TK]),
                bc_last(c.key[:, bass.ds(i * UN + h * KG, KG)], TK), ALU.is_equal).then_inc(hot_ready, 1)

        per_group = 1 if cnt is None else 3
        with dve.Fori(0, rounds) as q:
            with dve.If(rounds > 1):
                windows(dve, c, Chain(dve, table_steps, q * WINDOW_STEPS))
                gate(dve, c.passed)
            dve.end_ifs()
            dve.sem_inc(tables, 1)
            for h in range(BUFS):
                one_hot(h, q, 0)
            dve.wait_ge(zeroed, zeros)
            gate(dve, c.passed)

            def iteration(i, tiles):
                n = dve.snap(q * NG + i * RING)
                ch = Chain(dve, steps, n * per_group)
                for h in range(len(tiles)):
                    b = h % BUFS
                    g0 = dve.value_load(c.gs_i[0:1, bass.ds(i * RING + h, 1)], min_val=0, max_val=NPAD)
                    if cnt is not None:
                        dve.wait_ge(summed, n + (h + 1 + RING))
                        ch.then(dve.tensor_reduce(dsum[:, :], cnt_ps[b][0:1, :].rearrange("p (n r) -> p n r", r=NREL),
                                                  AX.X, ALU.add))
                        window = cnt[:, bass.ds(g0, GN)]
                        ch.then(dve.tensor_tensor(window, window, dsum[:, :], ALU.add))
                    if tiles is FULL:
                        one_hot((h + BUFS) % RING, q, i + (h + BUFS) // RING)
                    dve.wait_ge(mixed, n + (h + 1 + BUFS))
                    window = c.acc[:, bass.ds(g0, GN)]
                    ch.then(dve.tensor_tensor(window, window, mix_ps, ALU.add))
                    dve.sem_inc(added, 1)
                assert ch.n == per_group * len(tiles)
            by_chunk(dve, c, q, iteration, tail.dve_early, tail.dve_late)
        tail.end_dve(dve)


def plain_sum(nc, ctx, c, table, tail):
    tag = "r3"

    def sb(name, shape, dt=F32):
        return ctx.enter_context(nc.sbuf_tensor(f"{tag}_{name}", shape, dt))

    def sem(name):
        return ctx.enter_context(nc.semaphore(f"{tag}_{name}"))

    most = N // GN + 2
    g = Gathers(nc, ctx, c, tag, table, 1, most)
    summed = g.summed
    S = sb("S", [P, BUFS, KG, GN])
    hot_ready = sem("hot_ready")
    added = sem("added")
    steps, table_steps, setup, zeroed = sem("steps"), sem("table_steps"), sem("setup"), sem("zeroed")
    sum_ps = c.psum[0:2]
    block = ctx.enter_context(nc.Block())

    @block.sync
    def _(sync):
        tail.sync(sync, rounds_of(sync, c, 1, most))

    @block.scalar
    def _(act):
        g.first(act)
        zero(act, c, c.acc[:, :]).then_inc(zeroed, 1)
        rounds = rounds_of(act, c, 1, most)
        with act.Fori(0, rounds) as q:
            def iteration(i, tiles):
                if tiles is FULL:
                    for h in range(RING):
                        g.take(act, h, q, i + 1)
            by_chunk(act, c, q, iteration, tail.act_early, tail.act_late)
            g.again(act, q)
        tail.end_act(act, rounds)

    @block.gpsimd
    def _(pool):
        g.run(pool, None)

    @block.tensor
    def _(pe):
        g.start(pe)
        rounds = rounds_of(pe, c, 1, most)
        with pe.Fori(0, rounds) as q:
            pe.wait_ge(g.cleared, q + 1)
            gate(pe, c.passed)

            def iteration(i, tiles):
                n = pe.snap(q * NG + i * RING)
                for h in range(len(tiles)):
                    b = h % BUFS
                    pe.wait_ge(added, n + (h + 1))
                    pe.wait_ge(hot_ready, n + (h + 1))
                    g.wait_rows(pe, h, i, tiles)
                    for k in range(tiles[h]):
                        mm = pe.matmul(sum_ps[b][:, 0:GN], g.rows[:, h * KG + k, :], S[:, b, k, :], start=(k == 0),
                                       stop=(k == tiles[h] - 1))
                    mm.then_inc(summed, 1)
            by_chunk(pe, c, q, iteration, tail.pe_early, tail.pe_late)

    @block.vector
    def _(dve):
        dve.sem_inc(added, BUFS)
        tail.start_dve(dve)
        dve.memset(c.step_g[:, :], 0.0).then_inc(setup, 1)
        dve.wait_ge(setup, 1)
        rounds = rounds_of(dve, c, 1, most)

        def one_hot(h, q, i):
            dve.wait_ge(summed, q * NG + (i * RING + (h + 1 - BUFS + RING)))
            dve.tensor_tensor(
                S[:, h % BUFS, :, :], c.iota[:, 0:GN].unsqueeze(1).broadcast_to([P, KG, GN]),
                bc_last(c.key[:, bass.ds(i * UN + h * KG, KG)], GN), ALU.is_equal).then_inc(hot_ready, 1)

        per_table = 4
        with dve.Fori(0, rounds) as q:
            ch = Chain(dve, table_steps, q * per_table)
            ch.then(dve.tensor_scalar(c.gs[:, :], c.glo[:, :], c.step_g[:, 0:1], None, ALU.add))
            ch.then(dve.tensor_scalar(c.gs_i[:, :], c.gs[0:1, :], float(NPAD), None, ALU.min))
            ch.then(dve.tensor_tensor(by_group(c.key), by_group(c.node), bc_last(c.gs[:, :], KG), ALU.subtract))
            ch.then(dve.tensor_scalar(c.step_g[:, :], c.step_g[:, :], float(GN), None, ALU.add))
            assert ch.n == per_table
            for h in range(BUFS):
                one_hot(h, q, 0)
            dve.wait_ge(zeroed, 1)
            gate(dve, c.passed)

            def iteration(i, tiles):
                n = dve.snap(q * NG + i * RING)
                ch = Chain(dve, steps, n)
                for h in range(len(tiles)):
                    g0 = dve.value_load(c.gs_i[0:1, bass.ds(i * RING + h, 1)], min_val=0, max_val=NPAD)
                    dve.wait_ge(summed, n + (h + 1 + RING))
                    window = c.acc[:, bass.ds(g0, GN)]
                    ch.then(dve.tensor_tensor(window, window, sum_ps[h % BUFS][:, 0:GN], ALU.add))
                    dve.sem_inc(added, 1)
                    if tiles is FULL:
                        one_hot((h + BUFS) % RING, q, i + (h + BUFS) // RING)
            by_chunk(dve, c, q, iteration, tail.dve_early, tail.dve_late)
        tail.end_dve(dve)


def rows(table, ch):
    return table[ch.cols, :].rearrange("(a p) f -> p a f", p=P)


def load_rows(eng, to, table, ch, landed):
    if ch.last and table.shape[0] == N:
        part = LASTN % P
        eng.dma_start(to[:, 0, :], table[N - LASTN:N - part, :]).then_inc(landed, 16)
        eng.dma_start(to[0:part, 1, :], table[N - part:N, :]).then_inc(landed, 16)
    else:
        h = ch.b // 2
        for a in (0, h):
            eng.dma_start(to[:, a:a + h, :], rows(table, ch)[:, a:a + h, :]).then_inc(landed, 16)


def prefetched(sync, rounds, load, stores, settle):
    def store(*chunks):
        for one in stores:
            for ch in chunks:
                one(ch)

    with sync.Fori(0, rounds) as q:
        load(Chunk(q, 0, q * NCH))
        with sync.Fori(1, NCH - 2) as k:
            m = sync.snap(q * NCH + k)
            load(Chunk(q, k, m))
            store(Chunk(q, k - 1, m - 1))
            settle(Chunk(q, k - 1, m - 1))
        two = last_two(q)
        before = Chunk(q, NCH - 3, q * NCH + (NCH - 3))
        for ch in two:
            load(ch)
        store(before)
        settle(before)
        store(*two)
        settle(two[1], 2)


def blocks(ap):
    return ap.rearrange("p (a f) -> p a f", f=D)


def turn(pe, ch, to, of, ident):
    for a in range(ch.b):
        mm = pe.transpose(to[:, a * P:(a + 1) * P], of(a), ident[:, :])
    return mm


class Sets:

    def __init__(self, nc, ctx, tag):
        self.nc, self.ctx, self.tag = nc, ctx, tag

    def by_rows(self, name):
        return [self.sb(name + str(s), [P, b, D]) for s, b in enumerate((CB, LASTB))]

    def by_cols(self, name, parts=P):
        return [self.sb(name + str(s), [parts, b * P]) for s, b in enumerate((CB, LASTB))]

    def per_row(self, name, w):
        return [self.sb(name + str(s), [P, b, w]) for s, b in enumerate((CB, LASTB))]

    def sb(self, name, shape):
        return self.ctx.enter_context(self.nc.sbuf_tensor(f"{self.tag}_{name}", shape, F32))

    def sem(self, name):
        return self.ctx.enter_context(self.nc.semaphore(f"{self.tag}_{name}"))

    def sems(self, name):
        return [self.sem(f"{name}{s}") for s in range(2)]


class Tail1:

    def __init__(self, nc, ctx, c, x, x1_d, cnt):
        new = Sets(nc, ctx, "d1")
        self.c, self.x, self.x1_d, self.cnt = c, x, x1_d, cnt
        self.xr, self.yr = new.by_rows("xr"), new.by_rows("yr")
        self.xT = self.pre = self.yT = new.by_cols("xT")
        self.cntc = new.sb("cntc", [1, CH])
        self.x_in = new.sems("x_in")
        (self.x_turned, self.xT_done, self.selfed, self.pre_done, self.y_act, self.y_turned, self.y_done,
         self.out, self.stored, self.whole, self.cnt_done, self.counts, self.deg_in, self.degs, self.zeroed) = (
            new.sem(n) for n in ("x_turned", "xT_done", "selfed", "pre_done", "y_act", "y_turned", "y_done",
                                 "out", "stored", "whole", "cnt_done", "counts", "deg_in", "degs", "zeroed"))
        last = c.psum[7][:, 0:LASTB * P]
        self.PT = self.PS = [c.psum[6], last]
        self.PO = [c.psum[3], last]
        self.PD = [c.psum[2][:, 0:CB], c.psum[0][:, 0:LASTB]]

    def sync(self, sync, rounds):
        sync.sem_inc(self.x_turned, 1)
        sync.sem_inc(self.stored, 1)
        sync.wait_ge(self.zeroed, 1)

        def load(ch):
            sync.wait_ge(self.x_turned, ch.free)
            load_rows(sync, self.xr[ch.s], self.x, ch, self.x_in[ch.s])

        def store(ch):
            sync.wait_ge(self.y_done, ch.m + 2)
            sync.dma_start(rows(self.x1_d, ch), self.yr[ch.s][:, :, :]).then_inc(self.out, 16)

        def settle(ch, chunks=1):
            sync.wait_ge(self.out, ch.m * 16 + 16)
            sync.sem_inc(self.stored, chunks)
        prefetched(sync, rounds, load, [store], settle)

    def pe_early(self, pe, chunks):
        for ch in chunks:
            pe.wait_ge(self.x_in[ch.s], ch.i * 32 + 32)
            turn(pe, ch, self.PT[ch.s], lambda a: self.xr[ch.s][:, a, :], self.c.ident).then_inc(self.x_turned, 1)
        for ch in chunks:
            pe.wait_ge(self.xT_done, ch.m + 1)
            pe.matmul(self.PS[ch.s][:, :], self.c.SL[0][:, :], self.xT[ch.s][:, :], start=True, stop=True
                      ).then_inc(self.selfed, 1)

    def pe_late(self, pe, chunks, ahead):
        for ch in chunks:
            pe.wait_ge(self.cnt_done, ch.m + 1)
            for a in range(ch.b):
                mm = pe.matmul(self.PD[ch.s][:, a:a + 1], self.cntc[0:1, a * P:(a + 1) * P], self.c.one[:, :],
                               start=True, stop=True)
            mm.then_inc(self.counts, 1)
        for ch in chunks:
            pe.wait_ge(self.deg_in, ch.m + 1)
            pe.wait_ge(self.y_act, ch.m + 1)
            pe.wait_ge(self.y_done, ch.free)
            turn(pe, ch, self.PO[ch.s], lambda a: self.yT[ch.s][:, a * P:(a + 1) * P], self.c.ident
                 ).then_inc(self.y_turned, 1)
        self.pe_early(pe, ahead)

    def act_early(self, act, chunks):
        for ch in chunks:
            act.wait_ge(self.x_turned, ch.m + 2)
            act.copy(self.xT[ch.s][:, :], self.PT[ch.s][:, :]).then_inc(self.xT_done, 1)

    def act_late(self, act, chunks, ahead):
        for ch in chunks:
            act.wait_ge(self.whole, ch.m + 1)
            if ch.last:
                act.wait_ge(self.counts, ch.m)
            act.copy(self.cntc[:, 0:ch.n], self.cnt[:, ch.cols]).then_inc(self.cnt_done, 1)
        for ch in chunks:
            act.wait_ge(self.pre_done, ch.m + 1)
            act.activation(self.yT[ch.s][:, :], self.pre[ch.s][:, :], ACT.Relu, bias=self.c.B[0][:, 0:1]
                           ).then_inc(self.y_act, 1)
        self.act_early(act, ahead)

    def end_act(self, act, rounds):
        act.wait_ge(self.deg_in, rounds * NCH)
        act.activation(self.c.deg[:, :], self.c.deg[:, :], ACT.Sqrt).then_inc(self.degs, 1)

    def start_dve(self, dve):
        dve.sem_inc(self.y_done, 1)
        dve.memset(self.xr[1][:, :, :], 0.0).then_inc(self.zeroed, 1)

    def dve_early(self, dve, chunks):
        pass

    def dve_late(self, dve, chunks, ahead):
        dve.sem_inc(self.whole, len(chunks))
        for ch in chunks:
            dve.wait_ge(self.selfed, ch.m + 1)
            dve.tensor_tensor(self.pre[ch.s][:, :], self.PS[ch.s][:, :], self.c.acc[:, ch.cols], ALU.add
                              ).then_inc(self.pre_done, 1)
        for ch in chunks:
            dve.wait_ge(self.counts, ch.m + 1)
            dve.tensor_scalar(self.c.deg[:, ch.blocks], self.PD[ch.s], 1.0, None, ALU.max).then_inc(self.deg_in, 1)
        for ch in chunks:
            dve.wait_ge(self.y_turned, ch.m + 1)
            dve.wait_ge(self.stored, ch.free)
            dve.tensor_copy(self.yr[ch.s][:, :, :], blocks(self.PO[ch.s][:, :])).then_inc(self.y_done, 1)

    def end_dve(self, dve):
        dve.wait_ge(self.degs, 1)
        dve.reciprocal(self.c.dinv[:, :], self.c.deg[:, :]).then_inc(self.degs, 1)


class Tail2:

    def __init__(self, nc, ctx, c, x, x1_d, z_d, feat_d, h_d):
        new = Sets(nc, ctx, "d2")
        self.c, self.x, self.x1_d, self.z_d, self.feat_d, self.h_d = c, x, x1_d, z_d, feat_d, h_d
        self.x1r, self.xr, self.rr, self.zr, self.fp, self.fr, self.hr = (
            new.by_rows(n) for n in ("x1r", "xr", "rr", "zr", "fp", "fr", "hr"))
        self.xT, self.pre, self.yT, self.zT = (new.by_cols(n) for n in ("xT", "pre", "yT", "zT"))
        self.st, self.mv = new.per_row("st", 6), new.per_row("mv", 2)
        self.sd, self.rstd = new.per_row("sd", 1), new.per_row("rstd", 1)
        self.x1_in, self.x_in = new.sems("x1_in"), new.sems("x_in")
        (self.x_turned, self.xT_done, self.selfed, self.pre_done, self.y_act, self.y_turned,
         self.res_done, self.var_done, self.sd_done, self.z_done, self.z_turned, self.zT_done, self.f_mm, self.f_pre, self.f_done,
         self.h_done, self.out, self.stored, self.steps, self.zeroed) = (
            new.sem(n) for n in ("x_turned", "xT_done", "selfed", "pre_done", "y_act", "y_turned",
                                 "res_done", "var_done", "sd_done", "z_done", "z_turned", "zT_done", "f_mm", "f_pre", "f_done",
                                 "h_done", "out", "stored", "steps", "zeroed"))
        last = c.psum[7][:, 0:LASTB * P]
        self.PT = self.PS = [c.psum[6], last]
        self.PO = self.PF = [c.psum[4], last]
        self.PZ = [c.psum[5], last]

    def sync(self, sync, rounds):
        sync.sem_inc(self.x_turned, 1)
        sync.sem_inc(self.res_done, 1)
        sync.sem_inc(self.stored, 1)
        sync.wait_ge(self.zeroed, 1)

        def load(ch):
            sync.wait_ge(self.x_turned, ch.free)
            load_rows(sync, self.x1r[ch.s], self.x1_d, ch, self.x1_in[ch.s])
            sync.wait_ge(self.res_done, ch.free)
            load_rows(sync, self.xr[ch.s], self.x, ch, self.x_in[ch.s])

        def store_z(ch):
            sync.wait_ge(self.z_done, ch.m + 1)
            sync.dma_start(rows(self.z_d, ch), self.zr[ch.s][:, :, :]).then_inc(self.out, 16)

        def store_feat(ch):
            sync.wait_ge(self.f_done, ch.m + 1)
            sync.dma_start(rows(self.feat_d, ch), self.fr[ch.s][:, :, :]).then_inc(self.out, 16)

        def store_h(ch):
            sync.wait_ge(self.h_done, ch.m + 1)
            sync.dma_start(rows(self.h_d, ch), self.hr[ch.s][:, :, :]).then_inc(self.out, 16)

        def settle(ch, chunks=1):
            sync.wait_ge(self.out, ch.m * 48 + 48)
            sync.sem_inc(self.stored, chunks)
        prefetched(sync, rounds, load, [store_z, store_feat, store_h], settle)

    def pe_early(self, pe, chunks):
        c = self.c
        for ch in chunks:
            pe.wait_ge(self.x1_in[ch.s], ch.i * 32 + 32)
            turn(pe, ch, self.PT[ch.s], lambda a: self.x1r[ch.s][:, a, :], c.ident).then_inc(self.x_turned, 1)
        for ch in chunks:
            pe.wait_ge(self.xT_done, ch.m + 1)
            pe.matmul(self.PS[ch.s][:, :], c.SL[1][:, :], self.xT[ch.s][:, :], start=True, stop=True
                      ).then_inc(self.selfed, 1)

    def pe_late(self, pe, chunks, ahead):
        c = self.c
        for ch in chunks:
            pe.wait_ge(self.y_act, ch.m + 1)
            pe.wait_ge(self.f_pre, ch.free)
            turn(pe, ch, self.PO[ch.s], lambda a: self.yT[ch.s][:, a * P:(a + 1) * P], c.ident
                 ).then_inc(self.y_turned, 1)
        self.pe_early(pe, ahead)
        for ch in chunks:
            pe.wait_ge(self.z_done, ch.m + 1)
            turn(pe, ch, self.PZ[ch.s], lambda a: self.zr[ch.s][:, a, :], c.ident).then_inc(self.z_turned, 1)
        for ch in chunks:
            pe.wait_ge(self.zT_done, ch.m + 1)
            for a in range(ch.b):
                mm = pe.matmul(self.PF[ch.s][:, a * D:(a + 1) * D], self.zT[ch.s][:, a * P:(a + 1) * P], c.GW[0][:, :],
                               start=True, stop=True)
            mm.then_inc(self.f_mm, 1)

    def act_early(self, act, chunks):
        for ch in chunks:
            act.wait_ge(self.x_turned, ch.m + 2)
            act.copy(self.xT[ch.s][:, :], self.PT[ch.s][:, :]).then_inc(self.xT_done, 1)

    def act_late(self, act, chunks, ahead):
        for ch in chunks:
            act.wait_ge(self.pre_done, ch.m + 1)
            act.activation(self.yT[ch.s][:, :], self.pre[ch.s][:, :], ACT.Relu, bias=self.c.B[1][:, 0:1]
                           ).then_inc(self.y_act, 1)
        self.act_early(act, ahead)
        for ch in chunks:
            act.wait_ge(self.var_done, ch.m + 1)
            act.activation(self.sd[ch.s][:, :, :], self.mv[ch.s][:, :, 1:2], ACT.Sqrt, bias=self.c.eps[:, 0:1]
                           ).then_inc(self.sd_done, 1)
        for ch in chunks:
            act.wait_ge(self.z_turned, ch.m + 1)
            act.copy(self.zT[ch.s][:, :], self.PZ[ch.s][:, :]).then_inc(self.zT_done, 1)
        for ch in chunks:
            act.wait_ge(self.f_pre, ch.m + 2)
            act.wait_ge(self.stored, ch.free)
            act.activation(self.fr[ch.s][:, :, :], self.fp[ch.s][:, :, :], ACT.Relu).then_inc(self.f_done, 1)

    def end_act(self, act, rounds):
        pass

    def start_dve(self, dve):
        dve.sem_inc(self.f_pre, 1)
        dve.memset(self.xr[1][:, :, :], 0.0).then_inc(self.zeroed, 1)

    def dve_early(self, dve, chunks):
        pass

    def dve_late(self, dve, chunks, ahead):
        c = self.c
        for ch in chunks:
            dve.wait_ge(self.selfed, ch.m + 1)
            dve.tensor_tensor(self.pre[ch.s][:, :], self.PS[ch.s][:, :], c.acc[:, ch.cols], ALU.add
                              ).then_inc(self.pre_done, 1)
        for ch in chunks:
            dve.wait_ge(self.y_turned, ch.m + 1)
            dve.wait_ge(self.x_in[ch.s], ch.i * 32 + 32)
            dve.tensor_tensor(self.rr[ch.s][:, :, :], blocks(self.PO[ch.s][:, :]), self.xr[ch.s][:, :, :], ALU.add
                              ).then_inc(self.res_done, 1)
        steps = Chain(dve, self.steps, chunks[0].m * 4)
        for ch in chunks:
            dve.wait_ge(self.res_done, ch.m + 2)
            stats(dve, steps, c.passed, self.rr[ch.s], self.st[ch.s], self.mv[ch.s], ch.b)
            dve.sem_inc(self.var_done, 1)
        for ch in chunks:
            dve.wait_ge(self.sd_done, ch.m + 1)
            steps.then(dve.reciprocal(self.rstd[ch.s][:, :, :], self.sd[ch.s][:, :, :]))
            dve.wait_ge(self.stored, ch.free)
            normed(dve, steps, self.rr[ch.s], self.mv[ch.s], self.rstd[ch.s], self.zr[ch.s], ch.b)
            dve.sem_inc(self.z_done, 1)
        for ch in chunks:
            dve.wait_ge(self.f_mm, ch.m + 1)
            dve.tensor_tensor(self.fp[ch.s][:, :, :], blocks(self.PF[ch.s][:, :]),
                              c.GB[0][:, :].unsqueeze(1).broadcast_to([P, ch.b, D]), ALU.add).then_inc(self.f_pre, 1)
        for ch in chunks:
            dve.wait_ge(self.f_done, ch.m + 1)
            dve.tensor_tensor(self.hr[ch.s][:, :, :], self.fr[ch.s][:, :, :], bc_last(c.dinv[:, ch.blocks], D),
                              ALU.mult).then_inc(self.h_done, 1)
        assert steps.n == 4 * len(chunks)

    def end_dve(self, dve):
        pass


class Tail3:

    def __init__(self, nc, ctx, c, z_d, feat_d, out):
        new = Sets(nc, ctx, "d3")
        self.c, self.z_d, self.feat_d, self.result = c, z_d, feat_d, out
        self.fr, self.zr, self.ag, self.ur, self.rr, self.r2, self.o = (
            new.by_rows(n) for n in ("fr", "zr", "ag", "ur", "rr", "r2", "o"))
        self.aT, self.uT = new.by_cols("aT"), new.by_cols("uT")
        self.st, self.mv = new.per_row("st", 6), new.per_row("mv", 2)
        self.sd, self.rstd = new.per_row("sd", 1), new.per_row("rstd", 1)
        self.in_ = new.sems("in")
        (self.whole, self.aT_done, self.a_turned, self.u_done, self.u_turned, self.uT_done, self.v_mm,
         self.v_done, self.var_done, self.sd_done, self.o_done, self.out, self.stored, self.steps) = (
            new.sem(n) for n in ("whole", "aT_done", "a_turned", "u_done", "u_turned", "uT_done", "v_mm", "v_done",
                                 "var_done", "sd_done", "o_done", "out", "stored", "steps"))
        last = LASTB * P
        self.PA = self.PV = [c.psum[4], c.psum[6][:, 0:last]]
        self.PU = [c.psum[5], c.psum[7][:, 0:last]]

    def sync(self, sync, rounds):
        sync.sem_inc(self.v_done, 1)
        sync.sem_inc(self.stored, 1)

        def load(ch):
            sync.wait_ge(self.v_done, ch.free)
            load_rows(sync, self.fr[ch.s], self.feat_d, ch, self.in_[ch.s])
            load_rows(sync, self.zr[ch.s], self.z_d, ch, self.in_[ch.s])

        def store(ch):
            sync.wait_ge(self.o_done, ch.m + 1)
            o = self.o[ch.s]
            if ch.last:
                whole = N - LASTN % P
                sync.dma_start(self.result[N - LASTN:whole, :], o[:, 0, :]).then_inc(self.out, 16)
                sync.dma_start(self.result[whole:N, :], o[0:N - whole, 1, :]).then_inc(self.out, 16)
            else:
                for a in (0, CB // 2):
                    sync.dma_start(rows(self.result, ch)[:, a:a + CB // 2, :], o[:, a:a + CB // 2, :]
                                   ).then_inc(self.out, 16)

        def settle(ch, chunks=1):
            sync.wait_ge(self.out, ch.m * 32 + 32)
            sync.sem_inc(self.stored, chunks)
        prefetched(sync, rounds, load, [store], settle)

    def pe_early(self, pe, chunks):
        pass

    def pe_late(self, pe, chunks, ahead):
        c = self.c
        for ch in chunks:
            pe.wait_ge(self.aT_done, ch.m + 1)
            pe.wait_ge(self.v_done, ch.free)
            turn(pe, ch, self.PA[ch.s], lambda a: self.aT[ch.s][:, a * P:(a + 1) * P], c.ident
                 ).then_inc(self.a_turned, 1)
        for ch in chunks:
            pe.wait_ge(self.u_done, ch.m + 1)
            turn(pe, ch, self.PU[ch.s], lambda a: self.ur[ch.s][:, a, :], c.ident).then_inc(self.u_turned, 1)
        for ch in chunks:
            pe.wait_ge(self.uT_done, ch.m + 1)
            for a in range(ch.b):
                mm = pe.matmul(self.PV[ch.s][:, a * D:(a + 1) * D], self.uT[ch.s][:, a * P:(a + 1) * P], c.GW[1][:, :],
                               start=True, stop=True)
            mm.then_inc(self.v_mm, 1)

    def act_early(self, act, chunks):
        pass

    def act_late(self, act, chunks, ahead):
        for ch in chunks:
            act.wait_ge(self.whole, ch.m + 1)
            act.copy(self.aT[ch.s][:, :], self.c.acc[:, ch.cols]).then_inc(self.aT_done, 1)
        for ch in chunks:
            act.wait_ge(self.u_turned, ch.m + 1)
            act.copy(self.uT[ch.s][:, :], self.PU[ch.s][:, :]).then_inc(self.uT_done, 1)
        for ch in chunks:
            act.wait_ge(self.var_done, ch.m + 1)
            act.activation(self.sd[ch.s][:, :, :], self.mv[ch.s][:, :, 1:2], ACT.Sqrt, bias=self.c.eps[:, 0:1]
                           ).then_inc(self.sd_done, 1)

    def end_act(self, act, rounds):
        pass

    def start_dve(self, dve):
        pass

    def dve_early(self, dve, chunks):
        pass

    def dve_late(self, dve, chunks, ahead):
        c = self.c
        dve.sem_inc(self.whole, len(chunks))
        steps = Chain(dve, self.steps, chunks[0].m * 6)
        for ch in chunks:
            dve.wait_ge(self.a_turned, ch.m + 1)
            steps.then(dve.tensor_tensor(self.ag[ch.s][:, :, :], blocks(self.PA[ch.s][:, :]),
                                         bc_last(c.dinv[:, ch.blocks], D), ALU.mult))
            dve.wait_ge(self.in_[ch.s], ch.i * 64 + 64)
            dve.tensor_tensor(self.ur[ch.s][:, :, :], self.fr[ch.s][:, :, :], self.ag[ch.s][:, :, :], ALU.subtract
                              ).then_inc(self.u_done, 1)
        for ch in chunks:
            dve.wait_ge(self.v_mm, ch.m + 1)
            dve.tensor_tensor(self.rr[ch.s][:, :, :], blocks(self.PV[ch.s][:, :]), self.zr[ch.s][:, :, :], ALU.add
                              ).then_inc(self.v_done, 1)
        for ch in chunks:
            dve.wait_ge(self.v_done, ch.m + 2)
            steps.then(dve.tensor_tensor(self.r2[ch.s][:, :, :], self.rr[ch.s][:, :, :],
                                         c.GB[1][:, :].unsqueeze(1).broadcast_to([P, ch.b, D]), ALU.add))
            stats(dve, steps, c.passed, self.r2[ch.s], self.st[ch.s], self.mv[ch.s], ch.b)
            dve.sem_inc(self.var_done, 1)
        for ch in chunks:
            dve.wait_ge(self.sd_done, ch.m + 1)
            steps.then(dve.reciprocal(self.rstd[ch.s][:, :, :], self.sd[ch.s][:, :, :]))
            dve.wait_ge(self.stored, ch.free)
            normed(dve, steps, self.r2[ch.s], self.mv[ch.s], self.rstd[ch.s], self.o[ch.s], ch.b)
            dve.sem_inc(self.o_done, 1)
        assert steps.n == 6 * len(chunks)

    def end_dve(self, dve):
        pass


def stats(dve, steps, passed, r, st, mv, b):
    for a in range(b):
        ins = dve.bn_stats(st[:, a, :], r[:, a, :])
    steps.then(ins)
    gate(dve, passed)
    for a in range(b):
        ins = dve.bn_aggr(mv[:, a, :], st[:, a, :])
    steps.then(ins)


def normed(dve, steps, r, mv, rstd, z, b):
    for a in range(b):
        ins = dve.tensor_scalar(z[:, a, :], r[:, a, :], mv[:, a, 0:1], rstd[:, a, :], ALU.subtract, ALU.mult)
    steps.then(ins)


_INS = ['x', 'src', 'dst', 'edge_type_8', 'L0_gnn_w1', 'L0_gnn_sl1', 'L0_gnn_b1', 'L0_gnn_w2', 'L0_gnn_sl2',
        'L0_gnn_b2', 'L1_gnn_W1', 'L1_gnn_b1', 'L1_gnn_W2', 'L1_gnn_b2']


def kernel(**inputs):
    import numpy as _np
    import concourse.bacc as _bacc
    from concourse import mybir as _mybir
    from concourse.bass_utils import run_bass_kernel_spmd as _run

    nc = _bacc.Bacc("TRN2", target_bir_lowering=False, num_devices=1)
    arrays, args = {}, []
    for name in _INS:
        a = _np.ascontiguousarray(inputs[name])
        arrays[f"in_{name}_dram"] = a
        args.append(nc.dram_tensor(f"in_{name}_dram", a.shape, _mybir.dt.from_np(a.dtype), kind="ExternalInput").ap())
    o = nc.dram_tensor("out_0_dram", (N, D), _mybir.dt.float32, kind="ExternalOutput").ap()
    build(nc, *args, o)
    r = _run(nc, [arrays], core_ids=[0])
    return r.results[0]["out_0_dram"]
```
